# Optimizing a Trainium2 kernel written in Bass

```python
import numpy as np
import jax
import jax.numpy as jnp

def _softmax(x, axis=-1):
    return jax.nn.softmax(x, axis=axis)

def _gelu(x):
    return jax.nn.gelu(x, approximate=True)

def _silu(x):
    return jax.nn.silu(x)

def _sigmoid(x):
    return jax.nn.sigmoid(x)

def _layernorm(x, axis=-1, eps=1e-05):
    m = jnp.mean(x, axis=axis, keepdims=True)
    v = jnp.var(x, axis=axis, keepdims=True)
    return (x - m) / jnp.sqrt(v + eps)

def _scatter_add(tgt, idx, src, axis=0):
    return tgt.at[idx].add(src)

def _segment_sum(src, seg, n):
    return jax.ops.segment_sum(src, seg, n)
kernel_name = 'mk_macaron_d2_jaxref_r8_02d86d'

def setup_inputs(seed: int=0):
    np.random.seed(seed)
    _w = jnp.asarray

    def _L0_attn_setup():
        import jax, jax.numpy as jnp
        import numpy as np
        B, S, HID = (1, 256, 256)
        H, HKV, D = (16, 4, 128)
        BS, NSEL = (64, 16)
        THETA = 10000.0

        def _rope(x, cos, sin):
            c = cos[None, :, None, :]
            s_ = sin[None, :, None, :]
            x1, x2 = jnp.split(x, 2, axis=-1)
            return x * c + jnp.concatenate([-x2, x1], axis=-1) * s_
        key = jax.random.key(seed)
        ks = jax.random.split(key, 8)
        w = lambda k, shape, fan: jax.random.normal(k, shape, jnp.float32) * fan ** (-0.5)
        return {'hidden_states': jax.random.normal(ks[0], (B, S, HID), jnp.float32), 'Wq': w(ks[1], (H * D, HID), HID), 'Wk': w(ks[2], (HKV * D, HID), HID), 'Wv': w(ks[3], (HKV * D, HID), HID), 'Wo': w(ks[4], (HID, H * D), H * D), 'Wkc': w(ks[5], (D // 4, D), D), 'Wgslc': w(ks[6], (H, HID), HID), 'Wgswa': w(ks[7], (H, HID), HID)}
    _L0_attn_in = _L0_attn_setup()

    def _L0_ffn_setup():
        import jax, jax.numpy as jnp
        import numpy as np
        TOP_K = 8
        NEG_INF = -1000000000.0
        key = jax.random.key(seed)
        ks = jax.random.split(key, 6)
        B, S, H, I, E, G, GS = (1, 256, 256, 176, 64, 8, 8)
        sc = 0.02
        return {'hidden_states': jax.random.normal(ks[0], (B, S, H), jnp.float32), 'gate_w': jax.random.normal(ks[1], (E, H), jnp.float32) * sc, 'mask_up_w': jax.random.normal(ks[2], (G, H, GS), jnp.float32) * sc, 'gate_proj_w': jax.random.normal(ks[3], (G, I, H), jnp.float32) * sc, 'up_proj_w': jax.random.normal(ks[4], (G, I, H), jnp.float32) * sc, 'down_proj_w': jax.random.normal(ks[5], (G, H, I), jnp.float32) * sc, 'inv_map': jnp.arange(G * GS, dtype=jnp.int64).reshape(G, GS)}
    _L0_ffn_in = _L0_ffn_setup()

    def _L1_attn_setup():
        import math
        import jax
        import jax.numpy as jnp
        import numpy as np
        from jax import lax
        B_, L, D_MODEL = (2, 128, 256)
        D_STATE, D_CONV, EXPAND = (16, 4, 2)
        D_INNER = EXPAND * D_MODEL
        DT_RANK = math.ceil(D_MODEL / 16)

        def _silu(v):
            return v * jax.nn.sigmoid(v)

        def _mamba_forward(hidden_states, in_proj_w, conv_w, conv_b, x_proj_w, dt_proj_w, dt_proj_b, A_log, D, out_proj_w):
            b, l, _ = hidden_states.shape
            xz = jnp.einsum('bld,ed->bel', hidden_states, in_proj_w)
            x, z = (xz[:, :D_INNER, :], xz[:, D_INNER:, :])
            A = -jnp.exp(A_log.astype(jnp.float32))
            xp = jnp.pad(x, ((0, 0), (0, 0), (D_CONV - 1, 0)))
            x = lax.conv_general_dilated(xp, conv_w[:, None, :], window_strides=(1,), padding='VALID', dimension_numbers=('NCH', 'OIH', 'NCH'), feature_group_count=D_INNER)
            x = _silu(x + conv_b[None, :, None])
            x_dbl = jnp.einsum('bdl,kd->blk', x, x_proj_w)
            dt_lo = x_dbl[..., :DT_RANK]
            Bmat = x_dbl[..., DT_RANK:DT_RANK + D_STATE]
            Cmat = x_dbl[..., DT_RANK + D_STATE:]
            delta = jax.nn.softplus(jnp.einsum('blr,dr->bld', dt_lo, dt_proj_w) + dt_proj_b.astype(jnp.float32))
            xt = jnp.transpose(x, (2, 0, 1))
            dl = jnp.transpose(delta, (1, 0, 2))
            Bl = jnp.transpose(Bmat, (1, 0, 2))
            Cl = jnp.transpose(Cmat, (1, 0, 2))

            def step(h, inp):
                d_t, B_t, C_t, x_t = inp
                dA = jnp.exp(d_t[..., None] * A)
                h = h * dA + d_t[..., None] * B_t[:, None, :] * x_t[..., None]
                y_t = jnp.sum(h * C_t[:, None, :], axis=-1)
                return (h, y_t)
            h0 = jnp.zeros((b, D_INNER, D_STATE), jnp.float32)
            _, ys = lax.scan(step, h0, (dl, Bl, Cl, xt))
            y = jnp.transpose(ys, (1, 0, 2))
            y = y + jnp.transpose(x, (0, 2, 1)) * D[None, None, :]
            y = y * _silu(jnp.transpose(z, (0, 2, 1)))
            out = jnp.einsum('bld,ed->ble', y, out_proj_w)
            return out
        key = jax.random.key(seed)
        ks = jax.random.split(key, 8)
        hidden_states = jax.random.normal(ks[0], (B_, L, D_MODEL), jnp.float32)
        in_proj_w = jax.random.normal(ks[1], (2 * D_INNER, D_MODEL), jnp.float32) * D_MODEL ** (-0.5)
        conv_w = jax.random.normal(ks[2], (D_INNER, D_CONV), jnp.float32) * D_CONV ** (-0.5)
        conv_b = jnp.zeros((D_INNER,), jnp.float32)
        x_proj_w = jax.random.normal(ks[3], (DT_RANK + 2 * D_STATE, D_INNER), jnp.float32) * D_INNER ** (-0.5)
        dt_std = DT_RANK ** (-0.5)
        dt_proj_w = jax.random.uniform(ks[4], (D_INNER, DT_RANK), jnp.float32, minval=-dt_std, maxval=dt_std)
        dt = jnp.exp(jax.random.uniform(ks[5], (D_INNER,), jnp.float32) * (math.log(0.1) - math.log(0.001)) + math.log(0.001))
        dt = jnp.clip(dt, 0.0001)
        dt_proj_b = dt + jnp.log(-jnp.expm1(-dt))
        A_log = jnp.log(jnp.broadcast_to(jnp.arange(1, D_STATE + 1, dtype=jnp.float32), (D_INNER, D_STATE)))
        D = jnp.ones((D_INNER,), jnp.float32)
        out_proj_w = jax.random.normal(ks[6], (D_MODEL, D_INNER), jnp.float32) * D_INNER ** (-0.5)
        return {'hidden_states': hidden_states, 'in_proj_w': in_proj_w, 'conv_w': conv_w, 'conv_b': conv_b, 'x_proj_w': x_proj_w, 'dt_proj_w': dt_proj_w, 'dt_proj_b': dt_proj_b, 'A_log': A_log, 'D': D, 'out_proj_w': out_proj_w}
    _L1_attn_in = _L1_attn_setup()

    def _L1_ffn_setup():
        import jax, jax.numpy as jnp
        import numpy as np
        TOP_K = 2
        CAPACITY_FACTOR = 1.0

        def _ffn(x, w1, w2):
            h = x @ w1
            x1, x2 = jnp.split(h, 2, axis=-1)
            return x1 * jax.nn.silu(x2) @ w2
        key = jax.random.key(seed)
        ks = jax.random.split(key, 6)
        B, S, D, F, E_r, E_s = (4, 256, 256, 128, 7, 1)
        sc_in = 1.0 / np.sqrt(D)
        sc_mid = 1.0 / np.sqrt(F)
        return {'x': jax.random.normal(ks[0], (B, S, D), dtype=jnp.float32), 'gate_w': jax.random.normal(ks[1], (D, E_r), dtype=jnp.float32) * sc_in, 'expert_bias': jnp.zeros((E_r,), dtype=jnp.float32), 'shared_w1': jax.random.normal(ks[2], (E_s, D, 2 * F), dtype=jnp.float32) * sc_in, 'shared_w2': jax.random.normal(ks[3], (E_s, F, D), dtype=jnp.float32) * sc_mid, 'routed_w1': jax.random.normal(ks[4], (E_r, D, 2 * F), dtype=jnp.float32) * sc_in, 'routed_w2': jax.random.normal(ks[5], (E_r, F, D), dtype=jnp.float32) * sc_mid}
    _L1_ffn_in = _L1_ffn_setup()
    _d = {'L0_attn_hidden_states': _L0_attn_in['hidden_states'], 'L0_attn_Wq': _L0_attn_in['Wq'], 'L0_attn_Wk': _L0_attn_in['Wk'], 'L0_attn_Wv': _L0_attn_in['Wv'], 'L0_attn_Wo': _L0_attn_in['Wo'], 'L0_attn_Wkc': _L0_attn_in['Wkc'], 'L0_attn_Wgslc': _L0_attn_in['Wgslc'], 'L0_attn_Wgswa': _L0_attn_in['Wgswa'], 'L0_ffn_gate_w': _L0_ffn_in['gate_w'], 'L0_ffn_mask_up_w': _L0_ffn_in['mask_up_w'], 'L0_ffn_gate_proj_w': _L0_ffn_in['gate_proj_w'], 'L0_ffn_up_proj_w': _L0_ffn_in['up_proj_w'], 'L0_ffn_down_proj_w': _L0_ffn_in['down_proj_w'], 'L0_ffn_inv_map': _L0_ffn_in['inv_map'], 'L1_attn_in_proj_w': _L1_attn_in['in_proj_w'], 'L1_attn_conv_w': _L1_attn_in['conv_w'], 'L1_attn_conv_b': _L1_attn_in['conv_b'], 'L1_attn_x_proj_w': _L1_attn_in['x_proj_w'], 'L1_attn_dt_proj_w': _L1_attn_in['dt_proj_w'], 'L1_attn_dt_proj_b': _L1_attn_in['dt_proj_b'], 'L1_attn_A_log': _L1_attn_in['A_log'], 'L1_attn_D': _L1_attn_in['D'], 'L1_attn_out_proj_w': _L1_attn_in['out_proj_w'], 'L1_ffn_gate_w': _L1_ffn_in['gate_w'], 'L1_ffn_expert_bias': _L1_ffn_in['expert_bias'], 'L1_ffn_shared_w1': _L1_ffn_in['shared_w1'], 'L1_ffn_shared_w2': _L1_ffn_in['shared_w2'], 'L1_ffn_routed_w1': _L1_ffn_in['routed_w1'], 'L1_ffn_routed_w2': _L1_ffn_in['routed_w2']}
    _x0 = _d['L0_attn_hidden_states']
    _d['L0_attn_hidden_states'] = jax.random.normal(jax.random.fold_in(jax.random.key(seed), 1), (2, 1024, 256), dtype=_x0.dtype)
    del _x0
    return _d

def reference(L0_attn_hidden_states, L0_attn_Wq, L0_attn_Wk, L0_attn_Wv, L0_attn_Wo, L0_attn_Wkc, L0_attn_Wgslc, L0_attn_Wgswa, L0_ffn_gate_w, L0_ffn_mask_up_w, L0_ffn_gate_proj_w, L0_ffn_up_proj_w, L0_ffn_down_proj_w, L0_ffn_inv_map, L1_attn_in_proj_w, L1_attn_conv_w, L1_attn_conv_b, L1_attn_x_proj_w, L1_attn_dt_proj_w, L1_attn_dt_proj_b, L1_attn_A_log, L1_attn_D, L1_attn_out_proj_w, L1_ffn_gate_w, L1_ffn_expert_bias, L1_ffn_shared_w1, L1_ffn_shared_w2, L1_ffn_routed_w1, L1_ffn_routed_w2):

    def _L0_attn_ref(hidden_states, Wq, Wk, Wv, Wo, Wkc, Wgslc, Wgswa):
        import jax, jax.numpy as jnp
        import numpy as np
        B, S, HID = (1, 256, 256)
        H, HKV, D = (16, 4, 128)
        BS, NSEL = (64, 16)
        THETA = 10000.0

        def _rope(x, cos, sin):
            c = cos[None, :, None, :]
            s_ = sin[None, :, None, :]
            x1, x2 = jnp.split(x, 2, axis=-1)
            return x * c + jnp.concatenate([-x2, x1], axis=-1) * s_
        b, sl, _ = hidden_states.shape
        g_slc = jax.nn.sigmoid(hidden_states @ Wgslc.T)
        g_swa = jax.nn.sigmoid(hidden_states @ Wgswa.T)
        q = (hidden_states @ Wq.T).reshape(b, sl, H, D)
        k = (hidden_states @ Wk.T).reshape(b, sl, HKV, D)
        v = (hidden_states @ Wv.T).reshape(b, sl, HKV, D)
        inv_freq = 1.0 / THETA ** (jnp.arange(0, D, 2, dtype=jnp.float32) / D)
        t = jnp.arange(sl, dtype=jnp.float32)
        freqs = jnp.outer(t, inv_freq)
        emb = jnp.concatenate([freqs, freqs], axis=-1)
        cos, sin = (jnp.cos(emb), jnp.sin(emb))
        q = _rope(q, cos, sin)
        k = _rope(k, cos, sin)
        q = q.transpose(0, 2, 1, 3)
        k = jnp.repeat(k.transpose(0, 2, 1, 3), H // HKV, axis=1)
        v = jnp.repeat(v.transpose(0, 2, 1, 3), H // HKV, axis=1)
        nb = (sl + BS - 1) // BS
        kc = k @ Wkc.T
        pad = nb * BS - sl
        kc = jnp.pad(kc, ((0, 0), (0, 0), (0, pad), (0, 0)))
        kbm = kc.reshape(b, H, nb, BS, D // 4).mean(axis=3)
        qc = q @ Wkc.T
        bscores = jnp.einsum('bhsd,bhnd->bhsn', qc, kbm) / jnp.sqrt(jnp.float32(D // 4))
        pos_blk = jnp.arange(sl) // BS
        cmask = jnp.arange(nb)[None, :] <= pos_blk[:, None]
        bscores = jnp.where(cmask[None, None], bscores, -jnp.inf)
        topk = min(NSEL, nb)
        _, idx = jax.lax.top_k(bscores, topk)
        block_indices = jnp.sort(idx, axis=-1)
        scale = 1.0 / jnp.sqrt(jnp.float32(D))
        scores = jnp.einsum('bhsd,bhtd->bhst', q, k) * scale
        causal = jnp.tril(jnp.ones((sl, sl), bool))
        scores = jnp.where(causal[None, None], scores, -jnp.inf)
        attn = jnp.einsum('bhst,bhtd->bhsd', jax.nn.softmax(scores, axis=-1), v)
        g = (g_slc + g_swa).transpose(0, 2, 1)[..., None]
        out = (g * attn).transpose(0, 2, 1, 3).reshape(b, sl, H * D)
        return out @ Wo.T

    def _L0_ffn_ref(hidden_states, gate_w, mask_up_w, gate_proj_w, up_proj_w, down_proj_w, inv_map):
        import jax, jax.numpy as jnp
        import numpy as np
        TOP_K = 8
        NEG_INF = -1000000000.0
        B, S, H = hidden_states.shape
        x = hidden_states.reshape(-1, H)
        N = x.shape[0]
        E = gate_w.shape[0]
        scores = jax.nn.softmax(x @ gate_w.T, axis=-1)
        topk_w, topk_idx = jax.lax.top_k(scores, TOP_K)
        w_e = jnp.zeros((N, E), x.dtype).at[jnp.arange(N)[:, None], topk_idx].add(topk_w)
        flat = w_e[:, inv_map]
        scalar = flat.sum(-1)
        soft = jax.nn.softmax(jnp.where(flat == 0, NEG_INF, flat), axis=-1)
        xg = x[:, None, :] + jnp.einsum('ngi,ghi->ngh', soft, mask_up_w)
        g = jnp.einsum('ngh,gih->ngi', xg, gate_proj_w)
        u = jnp.einsum('ngh,gih->ngi', xg, up_proj_w)
        a = jax.nn.silu(g) * u
        d = jnp.einsum('ngi,ghi->ngh', a, down_proj_w)
        y = jnp.einsum('ng,ngh->nh', scalar, d)
        return y.reshape(B, S, H)

    def _L1_attn_ref(hidden_states, in_proj_w, conv_w, conv_b, x_proj_w, dt_proj_w, dt_proj_b, A_log, D, out_proj_w):
        import math
        import jax
        import jax.numpy as jnp
        import numpy as np
        from jax import lax
        B_, L, D_MODEL = (2, 128, 256)
        D_STATE, D_CONV, EXPAND = (16, 4, 2)
        D_INNER = EXPAND * D_MODEL
        DT_RANK = math.ceil(D_MODEL / 16)

        def _silu(v):
            return v * jax.nn.sigmoid(v)

        def _mamba_forward(hidden_states, in_proj_w, conv_w, conv_b, x_proj_w, dt_proj_w, dt_proj_b, A_log, D, out_proj_w):
            b, l, _ = hidden_states.shape
            xz = jnp.einsum('bld,ed->bel', hidden_states, in_proj_w)
            x, z = (xz[:, :D_INNER, :], xz[:, D_INNER:, :])
            A = -jnp.exp(A_log.astype(jnp.float32))
            xp = jnp.pad(x, ((0, 0), (0, 0), (D_CONV - 1, 0)))
            x = lax.conv_general_dilated(xp, conv_w[:, None, :], window_strides=(1,), padding='VALID', dimension_numbers=('NCH', 'OIH', 'NCH'), feature_group_count=D_INNER)
            x = _silu(x + conv_b[None, :, None])
            x_dbl = jnp.einsum('bdl,kd->blk', x, x_proj_w)
            dt_lo = x_dbl[..., :DT_RANK]
            Bmat = x_dbl[..., DT_RANK:DT_RANK + D_STATE]
            Cmat = x_dbl[..., DT_RANK + D_STATE:]
            delta = jax.nn.softplus(jnp.einsum('blr,dr->bld', dt_lo, dt_proj_w) + dt_proj_b.astype(jnp.float32))
            xt = jnp.transpose(x, (2, 0, 1))
            dl = jnp.transpose(delta, (1, 0, 2))
            Bl = jnp.transpose(Bmat, (1, 0, 2))
            Cl = jnp.transpose(Cmat, (1, 0, 2))

            def step(h, inp):
                d_t, B_t, C_t, x_t = inp
                dA = jnp.exp(d_t[..., None] * A)
                h = h * dA + d_t[..., None] * B_t[:, None, :] * x_t[..., None]
                y_t = jnp.sum(h * C_t[:, None, :], axis=-1)
                return (h, y_t)
            h0 = jnp.zeros((b, D_INNER, D_STATE), jnp.float32)
            _, ys = lax.scan(step, h0, (dl, Bl, Cl, xt))
            y = jnp.transpose(ys, (1, 0, 2))
            y = y + jnp.transpose(x, (0, 2, 1)) * D[None, None, :]
            y = y * _silu(jnp.transpose(z, (0, 2, 1)))
            out = jnp.einsum('bld,ed->ble', y, out_proj_w)
            return out
        return _mamba_forward(hidden_states, in_proj_w, conv_w, conv_b, x_proj_w, dt_proj_w, dt_proj_b, A_log, D, out_proj_w)

    def _L1_ffn_ref(x, gate_w, expert_bias, shared_w1, shared_w2, routed_w1, routed_w2):
        import jax, jax.numpy as jnp
        import numpy as np
        TOP_K = 2
        CAPACITY_FACTOR = 1.0

        def _ffn(x, w1, w2):
            h = x @ w1
            x1, x2 = jnp.split(h, 2, axis=-1)
            return x1 * jax.nn.silu(x2) @ w2
        B, S, D = x.shape
        E_r = gate_w.shape[1]
        T = B * S
        capacity = max(1, int(CAPACITY_FACTOR * T / E_r))
        flat_x = x.reshape(T, D)
        shared_sum = jax.vmap(_ffn, in_axes=(None, 0, 0))(flat_x, shared_w1, shared_w2).sum(0)
        gate_logits = flat_x @ gate_w + expert_bias
        aff = jax.nn.sigmoid(gate_logits)
        _, topk_idx = jax.lax.top_k(aff, TOP_K)
        mask = (topk_idx[:, :, None] == jnp.arange(E_r)[None, None, :]).any(axis=1)
        score = jnp.where(mask, aff, -1.0).T
        _, sel_idx = jax.lax.top_k(score, capacity)
        kept = jnp.take_along_axis(mask.T, sel_idx, axis=1)
        w = jnp.where(kept, jnp.take_along_axis(aff.T, sel_idx, axis=1), 0.0)
        inp = flat_x[sel_idx]
        out = jax.vmap(_ffn)(inp, routed_w1, routed_w2)
        routed_sum = jnp.zeros_like(flat_x).at[sel_idx].add(out * w[:, :, None])
        return (shared_sum + routed_sum).reshape(B, S, D)
    x = L0_attn_hidden_states
    x = x + 0.5 * _L0_ffn_ref(_layernorm(x, axis=-1), L0_ffn_gate_w, L0_ffn_mask_up_w, L0_ffn_gate_proj_w, L0_ffn_up_proj_w, L0_ffn_down_proj_w, L0_ffn_inv_map)
    x = x + _L0_attn_ref(_layernorm(x, axis=-1), L0_attn_Wq, L0_attn_Wk, L0_attn_Wv, L0_attn_Wo, L0_attn_Wkc, L0_attn_Wgslc, L0_attn_Wgswa)
    x = x + 0.5 * _L0_ffn_ref(_layernorm(x, axis=-1), L0_ffn_gate_w, L0_ffn_mask_up_w, L0_ffn_gate_proj_w, L0_ffn_up_proj_w, L0_ffn_down_proj_w, L0_ffn_inv_map)
    x = x + 0.5 * _L1_ffn_ref(_layernorm(x, axis=-1), L1_ffn_gate_w, L1_ffn_expert_bias, L1_ffn_shared_w1, L1_ffn_shared_w2, L1_ffn_routed_w1, L1_ffn_routed_w2)
    x = x + _L1_attn_ref(_layernorm(x, axis=-1), L1_attn_in_proj_w, L1_attn_conv_w, L1_attn_conv_b, L1_attn_x_proj_w, L1_attn_dt_proj_w, L1_attn_dt_proj_b, L1_attn_A_log, L1_attn_D, L1_attn_out_proj_w)
    x = x + 0.5 * _L1_ffn_ref(_layernorm(x, axis=-1), L1_ffn_gate_w, L1_ffn_expert_bias, L1_ffn_shared_w1, L1_ffn_shared_w2, L1_ffn_routed_w1, L1_ffn_routed_w2)
    return x

_drawn_inputs = setup_inputs


def setup_inputs(seed=0):
    import zlib

    import numpy as np

    out = dict(_drawn_inputs(seed))
    spreads = {'L1_attn_conv_b': (0.0, 0.1), 'L1_attn_D': (1.0, 0.2), 'L1_ffn_expert_bias': (0.0, 0.1)}
    factors = {'L0_ffn_gate_w': 4.587,
     'L0_ffn_mask_up_w': 8.0,
     'L0_ffn_gate_proj_w': 3.137,
     'L0_ffn_up_proj_w': 3.092,
     'L0_ffn_down_proj_w': 3.126}
    for name, (base, spread) in spreads.items():
        noise = np.random.default_rng([zlib.crc32(name.encode()), seed]).standard_normal(out[name].shape)
        drawn = base * np.exp(spread * noise) if base else spread * noise
        out[name] = jnp.asarray(drawn.astype(out[name].dtype))
    for name, factor in factors.items():
        out[name] = (out[name] * factor).astype(out[name].dtype)
    return out
```

```python
from contextlib import ExitStack

import numpy as np

import concourse.bass as bass
from concourse import mybir

F32 = mybir.dt.float32
BF16 = mybir.dt.bfloat16
I32 = mybir.dt.int32
F32R = mybir.dt.float32r
ALU = mybir.AluOpType
ACT = mybir.ActivationFunctionType
AX = mybir.AxisListType

P = 128
D = 256
KD = D // P
NB, L = 2, 1024
N = NB * L
NT = N // P
BLK = 512
TB = BLK // P
NBLK = N // BLK
EPS = 1e-5

STAGES = None
FIRST_STAGE_SEM = 120


class Pools:

    def __init__(self, nc, ctx, stage, first_sem=None):
        self.nc, self.ctx, self.stage = nc, ctx, stage
        self.next_sem, self.sems = first_sem, []
        if first_sem is not None:
            ctx.callback(self.clear_sems)

    def sb(self, name, shape, dt=F32):
        return self.ctx.enter_context(self.nc.sbuf_tensor(f"{self.stage}_{name}", shape, dt))

    def sem(self, name):
        if self.next_sem is None:
            return self.ctx.enter_context(self.nc.semaphore(f"{self.stage}_{name}"))
        sem = self.nc.alloc_semaphore(f"{self.stage}_{name}", self.next_sem)
        self.sems.append(sem)
        self.next_sem += 1
        return sem

    def clear_sems(self):
        self.nc.gpsimd.sem_clear(range(self.sems[0].num, self.sems[-1].num + 1))
        for sem in self.sems:
            self.nc.release_semaphore(sem)
        self.nc.all_engine_barrier(sem_only=True)


class Banks:

    def __init__(self, whole):
        self.whole = whole

    def __getitem__(self, j):
        if isinstance(j, slice):
            return [self[i] for i in range(j.start, j.stop)]
        return self.whole[:, j, :]

    def pair(self, j):
        return self.whole[:, j:j + 2, :]


def alone(eng, mark):
    eng.sem_inc(mark, 1)


class Split:

    def __init__(self, pool, name, shape):
        self.hi, self.lo = pool.sb(f"{name}_hi", shape, F32R), pool.sb(f"{name}_lo", shape, F32R)

    def __getitem__(self, at):
        return self.hi[at], self.lo[at]


def take_rest(eng, lo, value, hi):
    return eng.tensor_tensor(lo, value, hi.bitcast(F32), ALU.subtract)


def matmul_split(pe, out, lhs, rhs, start, stop):
    pe.matmul(out, lhs[0], rhs[0], start=start, stop=False)
    pe.matmul(out, lhs[0], rhs[1], start=False, stop=False)
    return pe.matmul(out, lhs[1], rhs[0], start=False, stop=stop)


class NormBlock:

    def __init__(self, pool, x, psum, consts):
        self.x, self.psum, self.c = x, psum, consts
        self.stats = pool.sb("bn_stats", [P, TB, 6])
        self.mv = pool.sb("mean_var", [P, TB, 2])
        self.std = pool.sb("std", [P, TB])
        self.rstd = pool.sb("rstd", [P, TB])
        self.xn = pool.sb("xn", [P, TB, D])
        self.xs = Split(pool, "xs", [P, 2, KD, BLK])
        self.s_bn = pool.sem("bn_stats")
        self.mark = pool.sem("norm_mark")
        self.s_var = pool.sem("var_ready")
        self.s_std = pool.sem("std_ready")
        self.s_rstd = pool.sem("rstd_ready")
        self.s_xn = pool.sem("xn_ready")
        self.s_tr = pool.sem("xn_turned")
        self.s_hi, self.s_lo = pool.sem("xs_hi"), pool.sem("xs_lo")

    def dve_stats(self, dve, n):
        for t in range(TB):
            ins = dve.bn_stats(self.stats[:, t, :], self.x[:, n * TB + t, :])
        ins.then_inc(self.s_bn, 1)
        dve.wait_ge(self.s_bn, n + 1)
        alone(dve, self.mark)
        for t in range(TB):
            ins = dve.bn_aggr(self.mv[:, t, :], self.stats[:, t, :])
        ins.then_inc(self.s_var, 1)

    def act_std(self, act, n):
        act.wait_ge(self.s_var, n + 1)
        act.activation(self.std[:, :], self.mv[:, :, 1], ACT.Sqrt, bias=self.c["eps"][:, 0:1]).then_inc(self.s_std, 1)

    def dve_apply(self, dve, n):
        dve.wait_ge(self.s_std, n + 1)
        dve.reciprocal(self.rstd[:, :], self.std[:, :]).then_inc(self.s_rstd, 1)
        dve.wait_ge(self.s_rstd, n + 1)
        if n > 0:
            dve.wait_ge(self.s_tr, n)
        for t in range(TB):
            ins = dve.tensor_scalar(self.xn[:, t, :], self.x[:, n * TB + t, :], self.mv[:, t, 0:1],
                                    self.rstd[:, t:t + 1], ALU.subtract, ALU.mult)
        ins.then_inc(self.s_xn, 1)

    def pe_turn(self, pe, n):
        pe.wait_ge(self.s_xn, n + 1)
        for k in range(KD):
            for t in range(TB):
                ins = pe.transpose(self.psum[:, k, t * P:(t + 1) * P], self.xn[:, t, k * P:(k + 1) * P],
                                   self.c["ident"][:, :])
        ins.then_inc(self.s_tr, 1)

    def act_xs(self, act, n):
        act.wait_ge(self.s_tr, n + 1)
        act.copy(self.xs.hi[:, n % 2, :, :], self.psum[:, :, :]).then_inc(self.s_hi, 1)

    def dve_xs(self, dve, n):
        dve.wait_ge(self.s_hi, n + 1)
        take_rest(dve, self.xs.lo[:, n % 2, :, :], self.psum[:, :, :], self.xs.hi[:, n % 2, :, :]).then_inc(self.s_lo, 1)


class NormAll:

    def __init__(self, pool, x, psum, consts, xn, xT):
        self.x, self.psum, self.c, self.xT = x, psum, consts, xT
        self.xn = [xn[:, i, :].rearrange("p (t d) -> p t d", t=TB) for i in range(2)]
        self.stats = pool.sb("bn_stats", [P, NT, 6])
        self.mv = pool.sb("mean_var", [P, NT, 2])
        self.std, self.rstd = pool.sb("std", [P, NT]), pool.sb("rstd", [P, NT])
        self.s_bn = pool.sem("bn_stats")
        self.mark = pool.sem("norm_mark")
        self.s_var = pool.sem("var_ready")
        self.s_std = pool.sem("std_ready")
        self.s_rstd = pool.sem("rstd_ready")
        self.s_xn = pool.sem("xn_ready")
        self.s_tr = pool.sem("xn_turned")
        self.s_act = pool.sem("xT_by_act")
        self.s_dve = pool.sem("xT_by_dve")

    def dve(self, dve):
        for t in range(NT):
            ins = dve.bn_stats(self.stats[:, t, :], self.x[:, t, :])
        ins.then_inc(self.s_bn, 1)
        dve.wait_ge(self.s_bn, 1)
        alone(dve, self.mark)
        for t in range(NT):
            ins = dve.bn_aggr(self.mv[:, t, :], self.stats[:, t, :])
        ins.then_inc(self.s_var, 1)
        dve.wait_ge(self.s_std, 1)
        dve.reciprocal(self.rstd[:, :], self.std[:, :]).then_inc(self.s_rstd, 1)
        dve.wait_ge(self.s_rstd, 1)
        for n in range(NBLK + 1):
            if n < NBLK:
                if n >= 2:
                    dve.wait_ge(self.s_tr, n - 1)
                for t in range(TB):
                    g = n * TB + t
                    ins = dve.tensor_scalar(self.xn[n % 2][:, t, :], self.x[:, g, :], self.mv[:, g, 0:1],
                                            self.rstd[:, g:g + 1], ALU.subtract, ALU.mult)
                ins.then_inc(self.s_xn, 1)
            if n > 0:
                m = n - 1
                cols = slice(m * BLK, (m + 1) * BLK)
                dve.wait_ge(self.s_tr, m + 1)
                if isinstance(self.xT, Split):
                    dve.wait_ge(self.s_act, m + 1)
                    take_rest(dve, self.xT.lo[:, :, cols], self.psum.pair(m % 2 * 2),
                              self.xT.hi[:, :, cols]).then_inc(self.s_dve, 1)
                else:
                    dve.tensor_copy(self.xT[:, 1, cols], self.psum[m % 2 * 2 + 1][:, :]).then_inc(self.s_dve, 1)

    def pe(self, pe, logits=None):
        for n in range(NBLK):
            pe.wait_ge(self.s_xn, n + 1)
            if n >= 2:
                pe.wait_ge(self.s_act, n - 1)
                pe.wait_ge(self.s_dve, n - 1)
            for k in range(KD):
                for t in range(TB):
                    ins = pe.transpose(self.psum[n % 2 * 2 + k][:, t * P:(t + 1) * P],
                                       self.xn[n % 2][:, t, k * P:(k + 1) * P], self.c["ident"][:, :])
            ins.then_inc(self.s_tr, 1)
            if logits and n > 0:
                logits.pe(pe, n - 1)
        if logits:
            logits.pe(pe, NBLK - 1)

    def act(self, act, logits=None):
        act.wait_ge(self.s_var, 1)
        act.activation(self.std[:, :], self.mv[:, :, 1], ACT.Sqrt, bias=self.c["eps"][:, 0:1]).then_inc(self.s_std, 1)
        for n in range(NBLK):
            cols = slice(n * BLK, (n + 1) * BLK)
            act.wait_ge(self.s_tr, n + 1)
            if isinstance(self.xT, Split):
                act.copy(self.xT.hi[:, :, cols], self.psum.pair(n % 2 * 2)).then_inc(self.s_act, 1)
            else:
                act.copy(self.xT[:, 0, cols], self.psum[n % 2 * 2][:, :]).then_inc(self.s_act, 1)
            if logits and n > 0:
                logits.act(act, n - 1)
        if logits:
            logits.act(act, NBLK - 1)

    def wait(self, eng):
        eng.wait_ge(self.s_act, NBLK)
        eng.wait_ge(self.s_dve, NBLK)


class Logits:

    def __init__(self, pool, psum, consts, norm, weight, rows, lT):
        self.psum, self.c, self.norm, self.w, self.rows = psum, consts, norm, weight, rows
        self.lT = lT
        self.out = psum[4]
        self.s_w = pool.sem("logits_w_ready")
        self.s_p = pool.sem("logitsT_products")
        self.s_c = pool.sem("logitsT_copied")
        self.s_t = pool.sem("logits_turned")

    def pe(self, pe, n):
        pe.wait_ge(self.norm.s_dve, n + 1)
        pe.wait_ge(self.s_w, 1)
        if n >= 2:
            pe.wait_ge(self.s_c, n - 1)
        for k in range(KD):
            ins = matmul_split(pe, self.psum[6 + n % 2][0:self.rows, :], self.w[:, k, :],
                               self.norm.xT[:, k, n * BLK:(n + 1) * BLK], k == 0, k == KD - 1)
        ins.then_inc(self.s_p, 1)

    def act(self, act, n):
        act.wait_ge(self.s_p, n + 1)
        act.copy(self.lT[:, n * BLK:(n + 1) * BLK], self.psum[6 + n % 2][0:self.rows, :]).then_inc(self.s_c, 1)

    def pe_turn(self, pe):
        pe.wait_ge(self.s_c, NBLK)
        for t in range(NT):
            ins = pe.transpose(self.out[:, t * self.rows:(t + 1) * self.rows], self.lT[:, t * P:(t + 1) * P],
                               self.c["ident"][0:self.rows, 0:self.rows])
        ins.then_inc(self.s_t, 1)


def grouped_ffn(nc, stage, x, psum, consts, w):
    G, GS, I = 8, 8, 176
    E, R = G * GS, G * I
    M = R // P
    with ExitStack() as ctx:
        pool = Pools(nc, ctx, stage, FIRST_STAGE_SEM)
        s_lp, s_lt, s_lg = pool.sem("logitsT_products"), pool.sem("logitT_ready"), pool.sem("logits_turned")
        norm = NormBlock(pool, x, psum.pair(0), consts)
        xs = norm.xs
        wgate, wup = Split(pool, "gate_w", [P, KD, R]), Split(pool, "up_w", [P, KD, R])
        wdown = Split(pool, "down_w", [P, M, D])
        raw_router, wrouter = pool.sb("router_w", [P, KD, E]), Split(pool, "router_w", [P, KD, E])
        raw_mask, wmask = pool.sb("mask_up_w", [P, KD, E]), Split(pool, "mask_up_w", [P, KD, E])
        c_hi = [pool.sb(f"{n}_of_mask_hi", [2 * E, R], F32R) for n in ("gate", "up")]
        c_lo = [pool.sb(f"{n}_of_mask_lo", [E, R], F32R) for n in ("gate", "up")]
        with ExitStack() as setup:
            early = Pools(nc, setup, stage)
            raw = [early.sb(f"raw_w{j}", [P, R * KD]) for j in range(2)]
            c_raw = [early.sb(f"raw_of_mask{j}", [E, R]) for j in range(2)]
        aT = Split(pool, "hiddenT", [P, M, BLK])
        pick = pool.sb("inv_map_onehot", [E, E])
        imap_i, imap_f = pool.sb("inv_map_i", [E, E], I32), pool.sb("inv_map_f", [E, E])
        spread = pool.sb("group_to_rows", [3 * G, R], BF16)
        logitT = pool.sb("router_logitsT", [E, BLK])
        logit = pool.sb("router_logits", [P, TB, E])
        prob = pool.sb("router_probs", [P, TB, E])
        rest = pool.sb("probs_beyond_top8", [P, TB, E])
        top = pool.sb("top8", [P, TB, 8])
        chosen = pool.sb("chosen", [P, TB, E])
        chosenT = pool.sb("chosenT", [E, BLK])
        row = pool.sb("row_stat", [P, 4, TB])
        flat = pool.sb("flat", [P, TB * G, GS])
        soft = pool.sb("soft", [P, TB * G, GS])
        grp = pool.sb("group_stat", [P, 5, TB * G])
        parts = pool.sb("scalar_parts", [P, TB, 3, G], BF16)
        softT = pool.sb("softT_hi_lo", [2 * E, 2, BLK], F32R)
        partsT = pool.sb("scalar_partsT", [3 * G, 2, BLK], BF16)
        sil = pool.sb("silu_gate", [P, 2, BLK])
        MB = 3
        mul = pool.sb("gate_up", [P, MB, BLK])

        pG, pU, pS, pY = psum[2:4], psum[4:6], psum[6], psum[7]
        pR = psum[0:2]
        s_w = [pool.sem(f"w{j}_loaded") for j in range(6)]
        W_ROUTER, W_MASK, W_GATE, W_UP, W_DOWN, W_MAP = range(6)
        s_wh = pool.sem("w_hi")
        s_wl = pool.sem("w_lo")
        s_wd = pool.sem("w_lo_by_dve")
        s_ah, s_al = pool.sem("hiddenT_hi"), pool.sem("hiddenT_lo")
        s_ch2, s_cl = pool.sem("mask_products_hi"), pool.sem("mask_products_lo")
        s_sh = pool.sem("softT_hi")
        s_cm = pool.sem("mask_products")
        s_ce = pool.sem("mask_products_copied")
        s_cz = pool.sem("mask_products_cut")
        s_sp = pool.sem("spread_built")
        s_pk = pool.sem("pick_built")
        s_zl = pool.sem("logits_less_max")
        s_ex = pool.sem("router_exp")
        s_ch = pool.sem("chosen_ready")
        s_ct = pool.sem("chosen_turned")
        s_cc = pool.sem("chosenT_ready")
        s_fl = pool.sem("flat_ready")
        s_fz = pool.sem("flat_less_max")
        s_fe = pool.sem("flat_exp")
        s_so = pool.sem("soft_ready")
        s_st = pool.sem("soft_turned")
        s_sa = pool.sem("softT_ready")
        s_sd = pool.sem("partsT_ready")
        s_v = pool.sem("router_dve_step")
        VSTEPS = 15
        s_g = pool.sem("gate_done")
        s_u = pool.sem("up_done")
        s_s = pool.sem("spread_done")
        s_si = pool.sem("silu_done")
        s_m = pool.sem("gate_up_done")
        s_a = pool.sem("hidden_done")
        s_y = pool.sem("down_done")
        s_x = pool.sem("residual_added")
        mark = pool.sem("mark")

        with nc.Block() as block:
            @block.sync
            def _(sp):
                sp.dma_start(raw_router[:, :, :], w["gate_w"].rearrange("(k p) e -> p k e", p=P)).then_inc(s_w[W_ROUTER], 16)
                sp.dma_start(imap_i[:, :], w["inv_map"]).then_inc(s_w[W_MAP], 16)
                sp.dma_start(raw_mask[:, :, :], w["mask_up_w"].rearrange("(k p) e -> p k e", p=P)).then_inc(s_w[W_MASK], 16)
                sp.dma_start(raw[0].rearrange("p (k r) -> p k r", k=KD), w["gate_proj_w"].rearrange("(k p) r -> p k r", p=P)).then_inc(s_w[W_GATE], 16)
                sp.dma_start(raw[1].rearrange("p (k r) -> p k r", k=KD), w["up_proj_w"].rearrange("(k p) r -> p k r", p=P)).then_inc(s_w[W_UP], 16)
                sp.wait_ge(s_wl, 3)
                sp.dma_start(raw[0].rearrange("p (m d) -> p m d", m=M), w["down_proj_w"].rearrange("(m p) d -> p m d", p=P)).then_inc(s_w[W_DOWN], 16)

            cuts = [(raw_router[:, :, :], wrouter, W_ROUTER), (raw_mask[:, :, :], wmask, W_MASK),
                    (raw[0].rearrange("p (k r) -> p k r", k=KD), wgate, W_GATE),
                    (raw[1].rearrange("p (k r) -> p k r", k=KD), wup, W_UP),
                    (raw[0].rearrange("p (m d) -> p m d", m=M), wdown, W_DOWN)]

            @block.gpsimd
            def _(pl):
                pl.memset(spread[:, :], 0.0).then_inc(s_sp, 1)
                v = spread[:, :].rearrange("r (g i) -> r g i", g=G)
                for part in range(3):
                    pl.wait_ge(s_sp, part + 1)
                    pl.affine_select(out=v, in_=v, pattern=[[-1, G], [0, I]], compare_op=ALU.not_equal, fill=1.0,
                                     base=-G * part, channel_multiplier=1).then_inc(s_sp, 1)
                def cut(j):
                    src, wt, _ = cuts[j]
                    pl.wait_ge(s_wh, j + 1)
                    take_rest(pl, wt.lo[:, :, :], src, wt.hi[:, :, :]).then_inc(s_wl, 1)

                for j in range(3):
                    cut(j)
                for j in range(2):
                    v = c_raw[j][:, :].rearrange("e (g i) -> e g i", g=G)
                    pl.wait_ge(s_ce, 3 * (j + 1))
                    pl.affine_select(out=v, in_=v, pattern=[[-GS, G], [0, I]], compare_op=ALU.is_ge, fill=0.0,
                                     base=0, channel_multiplier=1).then_inc(s_cz, 1)
                    pl.wait_ge(s_cz, 2 * j + 1)
                    pl.affine_select(out=v, in_=v, pattern=[[GS, G], [0, I]], compare_op=ALU.is_ge, fill=0.0,
                                     base=GS - 1, channel_multiplier=-1).then_inc(s_cz, 1)
                for j in range(2):
                    pl.wait_ge(s_ch2, 2 * j + 2)
                    take_rest(pl, c_lo[j][:, :], c_raw[j][:, :], c_hi[j][0:E, :]).then_inc(s_cl, 1)

                pl.wait_ge(s_cl, 2)
                pl.wait_ge(s_wd, 2)
                for n in range(NBLK):
                    for m in range(M):
                        i = n * M + m
                        pl.wait_ge(s_ah, i + 1)
                        take_rest(pl, aT.lo[:, m, :], mul[:, i % MB, :], aT.hi[:, m, :]).then_inc(s_al, 1)

            def router_dve(dve, n, step, first):
                def v(k):
                    return n * VSTEPS + k
                if step == 0:
                    norm.dve_stats(dve, n)
                elif step == 1:
                    norm.dve_apply(dve, n)
                elif step == 2:
                    norm.dve_xs(dve, n)
                elif step == 4:
                    dve.wait_ge(s_lg, n + 1)
                    lg = pR[1][:, 0:TB * E].rearrange("p (t e) -> p t e", t=TB)
                    dve.tensor_reduce(row[:, 0, :], lg, AX.X, ALU.max).then_inc(s_v, 1)
                    dve.wait_ge(s_v, v(1))
                    dve.tensor_tensor(logit[:, :, :], lg, row[:, 0, :].unsqueeze(2).broadcast_to([P, TB, E]),
                                      ALU.subtract).then_inc(s_zl, 1)
                elif step == 5:
                    dve.wait_ge(s_ex, n + 1)
                    dve.tensor_reduce(row[:, 1, :], prob[:, :, :], AX.X, ALU.add).then_inc(s_v, 1)
                    dve.wait_ge(s_v, v(2))
                    dve.reciprocal(row[:, 2, :], row[:, 1, :]).then_inc(s_v, 1)
                    dve.wait_ge(s_v, v(3))
                    dve.tensor_tensor(prob[:, :, :], prob[:, :, :], row[:, 2, :].unsqueeze(2).broadcast_to([P, TB, E]),
                                      ALU.mult).then_inc(s_v, 1)
                    dve.wait_ge(s_v, v(4))
                    alone(dve, mark)
                    for t in range(TB):
                        ins = dve.max(top[:, t, :], prob[:, t, :])
                    ins.then_inc(s_v, 1)
                    dve.wait_ge(s_v, v(5))
                    alone(dve, mark)
                    for t in range(TB):
                        ins = dve.match_replace(rest[:, t, :], top[:, t, :], prob[:, t, :], 0.0)
                    ins.then_inc(s_v, 1)
                    dve.wait_ge(s_v, v(6))
                    dve.tensor_tensor(chosen[:, :, :], prob[:, :, :], rest[:, :, :], ALU.subtract).then_inc(s_ch, 1)
                elif step == 7:
                    dve.wait_ge(s_fl, n + 1)
                    fl = pR[0][:, 0:TB * E].rearrange("p (g i) -> p g i", i=GS)
                    dve.tensor_scalar(flat[:, :, :], fl, 0.0, -1e9, ALU.is_equal, ALU.mult).then_inc(s_v, 1)
                    dve.wait_ge(s_v, v(7))
                    dve.tensor_tensor(flat[:, :, :], flat[:, :, :], fl, ALU.add).then_inc(s_v, 1)
                    dve.tensor_reduce(grp[:, 0, :], fl, AX.X, ALU.add).then_inc(s_v, 1)
                    dve.wait_ge(s_v, v(9))
                    dve.tensor_reduce(grp[:, 1, :], flat[:, :, :], AX.X, ALU.max).then_inc(s_v, 1)
                    dve.wait_ge(s_v, v(10))
                    dve.tensor_tensor(flat[:, :, :], flat[:, :, :],
                                      grp[:, 1, :].unsqueeze(2).broadcast_to([P, TB * G, GS]),
                                      ALU.subtract).then_inc(s_fz, 1)
                elif step == 8:
                    dve.wait_ge(s_fe, n + 1)
                    dve.tensor_reduce(grp[:, 2, :], soft[:, :, :], AX.X, ALU.add).then_inc(s_v, 1)
                    dve.wait_ge(s_v, v(11))
                    dve.reciprocal(grp[:, 3, :], grp[:, 2, :]).then_inc(s_v, 1)
                    dve.wait_ge(s_v, v(12))
                    dve.tensor_tensor(soft[:, :, :], soft[:, :, :],
                                      grp[:, 3, :].unsqueeze(2).broadcast_to([P, TB * G, GS]),
                                      ALU.mult).then_inc(s_so, 1)
                    sc = grp[:, 0, :].rearrange("p (t g) -> p t g", g=G)
                    r1 = grp[:, 4, :].rearrange("p (t g) -> p t g", g=G)
                    dve.tensor_scalar(parts[:, :, 0, :], sc, 0.5, None, ALU.mult).then_inc(s_v, 1)
                    dve.wait_ge(s_v, v(13))
                    dve.scalar_tensor_tensor(out=r1, in0=sc, scalar=0.5, in1=parts[:, :, 0, :], op0=ALU.mult,
                                             op1=ALU.subtract).then_inc(s_v, 1)
                    dve.wait_ge(s_v, v(14))
                    dve.tensor_copy(parts[:, :, 1, :], r1).then_inc(s_v, 1)
                    dve.wait_ge(s_v, v(15))
                    dve.tensor_tensor(parts[:, :, 2, :], r1, parts[:, :, 1, :], ALU.subtract).then_inc(s_so, 1)
                elif step == 9:
                    dve.wait_ge(s_st, n * 2 + 1)
                    if n >= 2:
                        dve.wait_ge(s_s, (n - 1) * M)
                    dve.tensor_copy(partsT[:, n % 2, :], pR[0][:, :].bitcast(BF16)[0:3 * G, 0:BLK]).then_inc(s_sd, 1)
                    dve.wait_ge(s_sh, n + 1)
                    take_rest(dve, softT[E:2 * E, n % 2, :], pR[1][0:E, :], softT[0:E, n % 2, :]).then_inc(s_sa, 1)

            def router_act(act, n, step, first):
                if step == 0:
                    norm.act_std(act, n)
                elif step == 2:
                    if n >= 2:
                        act.wait_ge(s_u, (n - 1) * M)
                    norm.act_xs(act, n)
                elif step == 3:
                    act.wait_ge(s_lp, n + 1)
                    act.copy(logitT[:, :], pR[0][0:E, :]).then_inc(s_lt, 1)
                elif step == 4:
                    act.wait_ge(s_zl, n + 1)
                    act.activation(prob[:, :, :], logit[:, :, :], ACT.Exp).then_inc(s_ex, 1)
                elif step == 6:
                    act.wait_ge(s_ct, n + 1)
                    act.copy(chosenT[:, :], pR[1][0:E, :]).then_inc(s_cc, 1)
                elif step == 7:
                    act.wait_ge(s_fz, n + 1)
                    act.activation(soft[:, :, :], flat[:, :, :], ACT.Exp).then_inc(s_fe, 1)
                elif step == 9:
                    act.wait_ge(s_st, n * 2 + 2)
                    if n >= 2:
                        act.wait_ge(s_u, (n - 1) * M)
                    act.copy(softT[0:E, n % 2, :], pR[1][0:E, :]).then_inc(s_sh, 1)

            def router_pe(pe, n, step, first):
                if step == 2:
                    if not first:
                        pe.wait_ge(s_sa, n)
                        pe.wait_ge(s_sd, n)
                    norm.pe_turn(pe, n)
                elif step == 3:
                    pe.wait_ge(norm.s_lo, n + 1)
                    if first:
                        pe.wait_ge(s_wl, 1)
                    for k in range(KD):
                        ins = matmul_split(pe, pR[0][0:E, :], wrouter[:, k, :], xs[:, n % 2, k, :], k == 0, k == KD - 1)
                    ins.then_inc(s_lp, 1)
                elif step == 4:
                    pe.wait_ge(s_lt, n + 1)
                    for t in range(TB):
                        ins = pe.transpose(pR[1][:, t * E:(t + 1) * E], logitT[:, t * P:(t + 1) * P],
                                           consts["ident"][0:E, 0:E])
                    ins.then_inc(s_lg, 1)
                elif step == 6:
                    pe.wait_ge(s_ch, n + 1)
                    alone(pe, mark)
                    for t in range(TB):
                        ins = pe.transpose(pR[1][0:E, t * P:(t + 1) * P], chosen[:, t, :], consts["ident"][:, :])
                    ins.then_inc(s_ct, 1)
                elif step == 7:
                    pe.wait_ge(s_cc, n + 1)
                    if first:
                        pe.wait_ge(s_pk, 3)
                    for t in range(TB):
                        ins = pe.matmul(pR[0][:, t * E:(t + 1) * E], chosenT[:, t * P:(t + 1) * P], pick[:, :],
                                        start=True, stop=True)
                    ins.then_inc(s_fl, 1)
                elif step == 9:
                    pe.wait_ge(s_so, n * 2 + 2)
                    alone(pe, mark)
                    pb = pR[0][:, :].bitcast(BF16)
                    for t in range(TB):
                        ins = pe.transpose(pb[0:3 * G, t * P:(t + 1) * P],
                                           parts[:, t, :, :].rearrange("p a g -> p (a g)"), consts["ident_bf"][:, :])
                    ins.then_inc(s_st, 1)
                    for t in range(TB):
                        ins = pe.transpose(pR[1][0:E, t * P:(t + 1) * P],
                                           soft[:, t * G:(t + 1) * G, :].rearrange("p g i -> p (g i)"),
                                           consts["ident"][:, :])
                    ins.then_inc(s_st, 1)

            ROUTER_STEPS = 10

            @block.tensor
            def _(pe):
                def down(n):
                    for t in range(TB):
                        bank = (pY, pS)[t % 2]
                        if t == 0:
                            pe.wait_ge(s_a, n * M + M)
                            pe.wait_ge(s_al, n * M + M)
                            pe.wait_ge(s_wd, 2)
                            if n > 0:
                                pe.wait_ge(s_x, n * TB)
                        if t >= 2:
                            pe.wait_ge(s_x, n * TB + t - 1)
                        for m in range(M):
                            ins = matmul_split(pe, bank[:, 0:D], aT[:, m, t * P:(t + 1) * P], wdown[:, m, :],
                                               m == 0, m == M - 1)
                        ins.then_inc(s_y, 1)

                def gate_up_of_x(n, m):
                    i = n * M + m
                    for wt, bank, read in ((wgate, pG[i % 2], s_si), (wup, pU[i % 2], s_m)):
                        if i >= 2:
                            pe.wait_ge(read, i - 1)
                        for k in range(KD):
                            matmul_split(pe, bank[:, :], wt[:, k, m * P:(m + 1) * P], xs[:, n % 2, k, :], k == 0, False)

                def experts(n):
                    for m in range(M):
                        i = n * M + m
                        rows = slice(m * P, (m + 1) * P)
                        if i >= 2:
                            gate_up_of_x(n, m)
                        if m == 0:
                            pe.wait_ge(s_sa, n + 1)
                            pe.wait_ge(s_sd, n + 1)
                        for j, (bank, done) in enumerate(((pG[i % 2], s_g), (pU[i % 2], s_u))):
                            pe.matmul(bank[:, :], c_hi[j][:, rows], softT[:, n % 2, :], start=False, stop=False)
                            pe.matmul(bank[:, :], c_lo[j][:, rows], softT[0:E, n % 2, :],
                                      start=False, stop=True).then_inc(done, 1)
                        if m == 0 and n > 0:
                            down(n - 1)
                        if m > 0:
                            pe.wait_ge(s_a, i)
                        elif n > 0:
                            pe.wait_ge(s_x, n * TB)
                        pe.matmul(pS[:, :], spread[:, rows], partsT[:, n % 2, :], start=True, stop=True).then_inc(s_s, 1)
                        if n + 1 < NBLK and m < ROUTER_STEPS:
                            router_pe(pe, n + 1, m, False)

                for step in range(ROUTER_STEPS):
                    if step == ROUTER_STEPS - 1:
                        pe.wait_ge(s_ce, 6)
                        gate_up_of_x(0, 0)
                        gate_up_of_x(0, 1)
                    router_pe(pe, 0, step, True)
                    if step == 4:
                        for j, wt in enumerate((wgate, wup)):
                            pe.wait_ge(*((s_wl, 3), (s_wd, 1))[j])
                            for c in range(3):
                                cols = slice(c * BLK, min((c + 1) * BLK, R))
                                bank = psum[2 + 3 * j + c]
                                for k in range(KD):
                                    ins = matmul_split(pe, bank[0:E, 0:cols.stop - cols.start], wmask[:, k, :],
                                                       wt[:, k, cols], k == 0, k == KD - 1)
                                ins.then_inc(s_cm, 1)
                pe.wait_ge(s_cl, 2)
                pe.wait_ge(s_sp, 4)
                for n in range(NBLK):
                    experts(n)
                down(NBLK - 1)

            @block.scalar
            def _(act):
                def cut(j):
                    src, wt, load = cuts[j]
                    act.wait_ge(s_w[load], 16)
                    act.copy(wt.hi[:, :, :], src).then_inc(s_wh, 1)

                def hidden_hi(i):
                    act.wait_ge(s_a, i + 1)
                    if i % M == 0 and i > 0:
                        act.wait_ge(s_y, i // M * TB)
                    act.copy(aT.hi[:, i % M, :], mul[:, i % MB, :]).then_inc(s_ah, 1)

                def experts(n):
                    for m in range(M):
                        i = n * M + m
                        act.wait_ge(s_g, i + 1)
                        if i >= 2:
                            act.wait_ge(s_m, i - 1)
                        act.activation(sil[:, i % 2, :], pG[i % 2][:, :], ACT.Silu).then_inc(s_si, 1)
                        if i == 1:
                            act.wait_ge(s_cl, 2)
                            act.wait_ge(s_wd, 2)
                        if m >= 1:
                            hidden_hi(i - 1)
                        if n + 1 < NBLK and m < ROUTER_STEPS:
                            router_act(act, n + 1, m, False)
                    hidden_hi(n * M + M - 1)

                cut(0)
                cut(1)
                for step in range(ROUTER_STEPS):
                    router_act(act, 0, step, True)
                    if step == 2:
                        cut(2)
                        cut(3)
                    if step in (6, 7):
                        j = step - 6
                        act.wait_ge(s_cz, 2 * j + 2)
                        act.copy(c_hi[j][0:E, :], c_raw[j][:, :]).then_inc(s_ch2, 1)
                        act.copy(c_hi[j][E:2 * E, :], c_raw[j][:, :]).then_inc(s_ch2, 1)
                    if step == ROUTER_STEPS - 1:
                        cut(4)
                    if step == 4:
                        for j in range(2):
                            for c in range(3):
                                cols = slice(c * BLK, min((c + 1) * BLK, R))
                                act.wait_ge(s_cm, 3 * j + c + 1)
                                act.copy(c_raw[j][:, cols], psum[2 + 3 * j + c][0:E, 0:cols.stop - cols.start]).then_inc(s_ce, 1)
                for n in range(NBLK):
                    experts(n)

            @block.vector
            def _(dve):
                dve.wait_ge(s_w[W_MAP], 16)
                dve.tensor_copy(imap_f[:, :], imap_i[:, :]).then_inc(s_pk, 2)
                dve.wait_ge(s_pk, 2)
                dve.tensor_scalar(pick[:, :], imap_f[:, :], consts["row_index"][0:E, 0:1], None,
                                  ALU.is_equal).then_inc(s_pk, 1)

                def experts(n):
                    for m in range(M):
                        i = n * M + m
                        dve.wait_ge(s_si, i + 1)
                        dve.wait_ge(s_u, i + 1)
                        if i >= MB:
                            dve.wait_ge(s_al, i - MB + 1)
                        hidden = mul[:, i % MB, :]
                        dve.tensor_tensor(hidden, sil[:, i % 2, :], pU[i % 2][:, :], ALU.mult).then_inc(s_m, 1)
                        dve.wait_ge(s_m, i + 1)
                        dve.wait_ge(s_s, i + 1)
                        dve.tensor_tensor(hidden, hidden, pS[:, :], ALU.mult).then_inc(s_a, 1)
                        if n + 1 < NBLK and m < ROUTER_STEPS:
                            router_dve(dve, n + 1, m, False)
                    for t in range(TB):
                        dve.wait_ge(s_y, n * TB + t + 1)
                        xt = x[:, n * TB + t, :]
                        dve.tensor_tensor(xt, xt, (pY, pS)[t % 2][:, 0:D], ALU.add).then_inc(s_x, 1)

                for step in range(ROUTER_STEPS):
                    router_dve(dve, 0, step, True)
                    if step in (2, 9):
                        j = 3 if step == 2 else 4
                        src, wt, _ = cuts[j]
                        dve.wait_ge(s_wh, j + 1)
                        take_rest(dve, wt.lo[:, :, :], src, wt.hi[:, :, :]).then_inc(s_wd, 1)
                for n in range(NBLK):
                    experts(n)


def routed_ffn(nc, stage, x, psum, consts, w):
    ER, F = 7, 128
    EX = ER + 1
    CAP = N // ER
    R = NT * ER
    BITS = 30
    STEP = 3
    TRIALS = (1 << STEP) - 1
    ROUNDS = BITS // STEP
    with ExitStack() as ctx:
        pool = Pools(nc, ctx, stage, FIRST_STAGE_SEM)
        xT = Split(pool, "xT", [P, KD, N])
        norm = NormAll(pool, x, psum, consts, pool.sb("xn", [P, 2, TB * D]), xT)
        EE = ER + ER % 2
        raw_gate, wgate = pool.sb("gate_w", [P, KD, EE]), Split(pool, "gate_w", [P, KD, EE])
        logits = Logits(pool, psum, consts, norm, wgate, EE, pool.sb("logitsT", [EE, N]))
        bias = pool.sb("expert_bias", [P, ER])
        raw_w1 = [pool.sb(f"w1_{j}", [P, KD, 2 * F]) for j in range(2)]
        raw_w2 = [pool.sb(f"w2_{j}", [P, D]) for j in range(2)]
        w1 = [Split(pool, f"w1_{j}", [P, KD, 2 * F]) for j in range(2)]
        w2 = [Split(pool, f"w2_{j}", [P, D]) for j in range(2)]
        aff = pool.sb("affinity", [P, NT, ER])
        above = pool.sb("above", [P, NT, ER, ER])
        equal = pool.sb("equal", [P, NT, ER, ER])
        lower = pool.sb("lower_index", [P, ER, ER])
        rank = pool.sb("rank", [P, NT, ER])
        asked = pool.sb("asked", [P, NT, ER])
        askT = pool.sb("askedT", [R, P])
        same_f, same = pool.sb("same_expert_f", [R, R]), pool.sb("same_expert", [R, R], BF16)
        before_f, before = pool.sb("earlier_tile_f", [R, R]), pool.sb("earlier_tile", [R, R], BF16)
        bits = pool.sb("trial_bits", [R, TRIALS], I32)
        floor = pool.sb("threshold", [R, 1], I32)
        trial = pool.sb("trial", [R, TRIALS], I32)
        passed, best = pool.sb("passed", [R, TRIALS]), pool.sb("best_passed", [R, 1])
        hits = pool.sb("hits", [R, TRIALS, P])
        count = pool.sb("count", [R, TRIALS], BF16)
        over, ties = pool.sb("over", [R, P]), pool.sb("ties", [R, P])
        nover, nties = pool.sb("n_over", [R, 1], BF16), pool.sb("n_ties", [R, 1], BF16)
        order, room = pool.sb("tie_order", [R, P]), pool.sb("room", [R, 1])
        kept = pool.sb("kept", [R, P])
        weight = pool.sb("weight", [P, NT, EX])
        sil = pool.sb("silu", [P, 2, BLK])
        hidden_f = pool.sb("hidden", [P, 2, BLK])
        hT = Split(pool, "hiddenT", [P, 2, BLK])

        pL, pC, pH, pV, pO = psum[4], psum[5], psum[4:6], psum[6:8], psum[0:2]
        s_w = pool.sem("router_w_loaded")
        s_w1 = [pool.sem(f"w1_{j}_loaded") for j in range(2)]
        s_w2 = [pool.sem(f"w2_{j}_loaded") for j in range(2)]
        s_gz = pool.sem("gate_w_padded")
        s_gh = pool.sem("gate_w_hi")
        s_ch = [pool.sem(f"w_{j}_hi") for j in range(2)]
        s_cl = [pool.sem(f"w_{j}_lo") for j in range(2)]
        s_lc = pool.sem("logits_taken")
        s_af = pool.sem("affinity_ready")
        s_lo = pool.sem("lower_index_built")
        s_v = pool.sem("router_dve_step")
        s_at = pool.sem("asked_turned")
        s_bit = pool.sem("bits_moved")
        s_be = pool.sem("best_ready")
        s_tr = pool.sem("trial_ready")
        s_cn = pool.sem("count_ready")
        s_su = pool.sem("counts_summed")
        s_ps = pool.sem("passed_ready")
        s_th = pool.sem("threshold_ready")
        s_k = pool.sem("kept_ready")
        s_kt = pool.sem("kept_turned")
        s_wt = pool.sem("weight_ready")
        s_h = pool.sem("up_products")
        s_si = pool.sem("silu_done")
        s_hf = pool.sem("hidden_ready")
        s_hh, s_hT = pool.sem("hiddenT_hi"), pool.sem("hiddenT_lo")
        s_o = pool.sem("down_products")
        s_x = pool.sem("residual_added")
        mark = pool.sem("mark")
        UNITS = 2 * NBLK
        VN = 8

        def steps(eng, unit, cut):
            def step(n, last):
                for k in range(UNITS):
                    unit(n, k)
                    if k == 1:
                        cut(n, 1)
                    if k == NBLK + 1 and not last:
                        cut(n + 1, 0)

            step(0, False)
            with eng.Fori(1, EX // 2 - 1) as n:
                step(n, False)
            step(EX // 2 - 1, True)

        with nc.Block() as block:
            @block.sync
            def _(sp):
                sp.dma_start(raw_gate[:, :, 0:ER], w["gate_w"].rearrange("(k p) e -> p k e", p=P)).then_inc(s_w, 16)
                sp.dma_start(bias[:, :], w["expert_bias"]).then_inc(s_w, 16)
                sp.dma_start(same_f[:, :], w["same_expert"]).then_inc(s_w, 16)
                sp.dma_start(before_f[:, :], w["earlier_tile"]).then_inc(s_w, 16)

                def load(n, j, first):
                    if not first:
                        sp.wait_ge(s_cl[j], n * 2)
                    sp.dma_start(raw_w1[j][:, :, :], w["w1"][bass.ds(n * 2 * D + j * D, D), :]
                                 .rearrange("(k p) f -> p k f", p=P)).then_inc(s_w1[j], 16)
                    sp.dma_start(raw_w2[j][:, :], w["w2"][bass.ds(n * 2 * F + j * F, F), :]).then_inc(s_w2[j], 16)

                load(0, 0, True)
                load(0, 1, True)
                with sp.Fori(1, EX // 2) as n:
                    load(n, 0, False)
                    load(n, 1, False)

            @block.gpsimd
            def _(pl):
                pl.memset(raw_gate[:, :, ER:EE], 0.0).then_inc(s_gz, 1)
                pl.memset(lower[:, :, :], 1.0).then_inc(s_lo, 1)
                pl.wait_ge(s_lo, 1)
                pl.affine_select(out=lower[:, :, :], in_=lower[:, :, :], pattern=[[1, ER], [-1, ER]],
                                 compare_op=ALU.is_gt, fill=0.0, base=0, channel_multiplier=0).then_inc(s_lo, 1)
                pl.wait_ge(s_gh, 1)
                take_rest(pl, wgate.lo[:, :, :], raw_gate[:, :, :], wgate.hi[:, :, :]).then_inc(logits.s_w, 1)

                def cut(n, j):
                    pl.wait_ge(s_ch[j], n * 2 + 2)
                    take_rest(pl, w1[j].lo[:, :, :], raw_w1[j][:, :, :], w1[j].hi[:, :, :]).then_inc(s_cl[j], 1)
                    take_rest(pl, w2[j].lo[:, :], raw_w2[j][:, :], w2[j].hi[:, :]).then_inc(s_cl[j], 1)

                def hidden_lo(n, k):
                    pl.wait_ge(s_hh, n * UNITS + k + 1)
                    take_rest(pl, hT.lo[:, k % 2, :], hidden_f[:, k % 2, :], hT.hi[:, k % 2, :]).then_inc(s_hT, 1)

                cut(0, 0)
                steps(pl, hidden_lo, cut)

            @block.scalar
            def _(act):
                act.wait_ge(s_w, 64)
                act.wait_ge(s_gz, 1)
                act.copy(wgate.hi[:, :, :], raw_gate[:, :, :]).then_inc(s_gh, 1)
                norm.act(act, logits)

                def cut(n, j):
                    act.wait_ge(s_w1[j], n * 16 + 16)
                    act.wait_ge(s_w2[j], n * 16 + 16)
                    if not isinstance(n, int) or n > 0:
                        act.wait_ge(s_o, (n * UNITS - UNITS + (j + 1) * NBLK) * 2)
                    act.copy(w1[j].hi[:, :, :], raw_w1[j][:, :, :]).then_inc(s_ch[j], 1)
                    act.copy(w2[j].hi[:, :], raw_w2[j][:, :]).then_inc(s_ch[j], 1)

                cut(0, 0)
                act.wait_ge(s_lc, 1)
                act.activation(aff[:, :, :], aff[:, :, :], ACT.Sigmoid).then_inc(s_af, 1)

                def unit(n, k):
                    first = isinstance(n, int) and n == 0 and k < 2
                    act.wait_ge(s_h, n * UNITS + k + 1)
                    if not first:
                        act.wait_ge(s_hf, n * UNITS + k - 1)
                    act.activation(sil[:, k % 2, :], pV[k % 2][:, :], ACT.Silu).then_inc(s_si, 1)
                    act.wait_ge(s_hf, n * UNITS + k + 1)
                    if not first:
                        act.wait_ge(s_o, (n * UNITS + k - 1) * 2)
                    act.copy(hT.hi[:, k % 2, :], hidden_f[:, k % 2, :]).then_inc(s_hh, 1)

                steps(act, unit, cut)

            @block.tensor
            def _(pe):
                norm.pe(pe, logits)
                logits.pe_turn(pe)
                pe.wait_ge(s_v, VN)
                pe.transpose(pL[0:R, 0:P], asked[:, :, :].rearrange("p t e -> p (t e)"),
                             consts["ident"][:, :]).then_inc(s_at, 1)
                with pe.Fori(0, ROUNDS) as b:
                    pe.wait_ge(s_cn, (b + 1) * TRIALS)
                    alone(pe, mark)
                    pe.matmul(pC[0:R, 0:TRIALS], same[:, :], count[:, :], start=True, stop=True).then_inc(s_su, 1)
                pe.wait_ge(s_k, 4)
                pe.matmul(pC[0:R, 0:1], same[:, :], nover[:, :], start=True, stop=False)
                pe.matmul(pC[0:R, 0:1], before[:, :], nties[:, :], start=False, stop=True).then_inc(s_su, 1)
                pe.wait_ge(s_k, 7)
                pe.transpose(pL[:, 0:R], kept[:, :], consts["ident"][0:R, 0:R]).then_inc(s_kt, 1)

                def up(n, k):
                    j, blk = k // NBLK, k % NBLK
                    if blk == 0:
                        pe.wait_ge(s_cl[j], n * 2 + 2)
                    if not (isinstance(n, int) and n == 0 and k < 2):
                        pe.wait_ge(s_hf, n * UNITS + k - 1)
                    for bank, c in ((pH[k % 2], 0), (pV[k % 2], 1)):
                        for kk in range(KD):
                            ins = matmul_split(pe, bank[:, :], w1[j][:, kk, c * F:(c + 1) * F],
                                               xT[:, kk, blk * BLK:(blk + 1) * BLK], kk == 0, kk == KD - 1)
                    ins.then_inc(s_h, 1)

                def down(n, k):
                    j = (k % UNITS) // NBLK
                    pe.wait_ge(s_hT, n * UNITS + k + 1)
                    for h in range(2):
                        if not (isinstance(n, int) and n == 0 and k == 0):
                            pe.wait_ge(s_x, (n * UNITS + k) * TB - 2 + 2 * h)
                        for t in range(2):
                            ins = matmul_split(pe, pO[h][:, t * D:(t + 1) * D],
                                               hT[:, k % 2, (2 * h + t) * P:(2 * h + t + 1) * P], w2[j][:, :],
                                               True, True)
                        ins.then_inc(s_o, 1)

                def unit(n, k):
                    up(n, k)
                    if not (isinstance(n, int) and n == 0 and k == 0):
                        down(n, k - 1)

                pe.wait_ge(s_kt, 1)
                pe.wait_ge(s_wt, 2)
                steps(pe, unit, lambda n, j: None)
                down(EX // 2 - 1, UNITS - 1)

            @block.vector
            def _(dve):
                norm.dve(dve)
                dve.wait_ge(s_w, 64)
                dve.wait_ge(logits.s_t, 1)
                dve.tensor_tensor(aff[:, :, :], pL[:, 0:NT * EE].rearrange("p (t e) -> p t e", e=EE)[:, :, 0:ER],
                                  bias[:, :].unsqueeze(1).broadcast_to([P, NT, ER]), ALU.add).then_inc(s_lc, 1)
                dve.wait_ge(s_af, 1)
                of_k = aff[:, :, :].unsqueeze(2).broadcast_to([P, NT, ER, ER])
                of_j = aff[:, :, :].unsqueeze(3).broadcast_to([P, NT, ER, ER])
                dve.tensor_tensor(above[:, :, :, :], of_k, of_j, ALU.is_gt).then_inc(s_v, 1)
                dve.tensor_tensor(equal[:, :, :, :], of_k, of_j, ALU.is_equal).then_inc(s_v, 1)
                dve.wait_ge(s_v, 2)
                dve.wait_ge(s_lo, 2)
                eq = equal[:, :, :, :].rearrange("p t j k -> p t (j k)")
                dve.tensor_tensor(eq, eq, lower[:, :, :].rearrange("p j k -> p (j k)").unsqueeze(1)
                                  .broadcast_to([P, NT, ER * ER]), ALU.mult).then_inc(s_v, 1)
                dve.wait_ge(s_v, 3)
                dve.tensor_tensor(equal[:, :, :, :], equal[:, :, :, :], above[:, :, :, :], ALU.add).then_inc(s_v, 1)
                dve.wait_ge(s_v, 4)
                dve.tensor_reduce(rank[:, :, :], equal[:, :, :, :], AX.X, ALU.add).then_inc(s_v, 1)
                dve.tensor_copy(same[:, :], same_f[:, :]).then_inc(s_v, 1)
                dve.tensor_copy(before[:, :], before_f[:, :]).then_inc(s_v, 1)
                dve.wait_ge(s_v, 7)
                dve.scalar_tensor_tensor(out=asked[:, :, :], in0=rank[:, :, :], scalar=1.5, in1=aff[:, :, :],
                                         op0=ALU.is_lt, op1=ALU.mult).then_inc(s_v, 1)
                for t in range(TRIALS):
                    dve.memset(bits[:, t:t + 1], (t + 1) << (BITS - STEP)).then_inc(s_bit, 1)
                dve.memset(floor[:, :], 0).then_inc(s_th, 1)
                dve.wait_ge(s_at, 1)
                dve.tensor_copy(askT[:, :], pL[0:R, 0:P]).then_inc(s_k, 1)
                dve.wait_ge(s_k, 1)
                with dve.Fori(0, ROUNDS) as b:
                    dve.wait_ge(s_bit, b + TRIALS)
                    dve.wait_ge(s_th, b + 1)
                    dve.tensor_tensor(trial[:, :], bits[:, :], floor[:, :].broadcast_to([R, TRIALS]),
                                      ALU.bitwise_or).then_inc(s_tr, 1)
                    dve.wait_ge(s_tr, b + 1)
                    alone(dve, mark)
                    for t in range(TRIALS):
                        dve.tensor_scalar(hits[:, t, :], askT[:, :], trial[:, t:t + 1].bitcast(F32), None, ALU.is_ge,
                                          ALU.add, accum_out=count[:, t:t + 1]).then_inc(s_cn, 1)
                    dve.tensor_scalar(bits[:, :], bits[:, :], STEP, None, ALU.logical_shift_right).then_inc(s_bit, 1)
                    dve.wait_ge(s_su, b + 1)
                    dve.scalar_tensor_tensor(out=passed[:, :], in0=pC[0:R, 0:TRIALS], scalar=CAP - 0.5,
                                             in1=trial[:, :].bitcast(F32), op0=ALU.is_ge, op1=ALU.mult).then_inc(s_ps, 1)
                    dve.wait_ge(s_ps, b + 1)
                    dve.tensor_reduce(best[:, :], passed[:, :], AX.X, ALU.max).then_inc(s_be, 1)
                    dve.wait_ge(s_be, b + 1)
                    dve.tensor_tensor(floor[:, :].bitcast(F32), floor[:, :].bitcast(F32), best[:, :],
                                      ALU.max).then_inc(s_th, 1)
                dve.wait_ge(s_th, ROUNDS + 1)
                th = floor[:, :].bitcast(F32)
                dve.tensor_scalar(over[:, :], askT[:, :], th, None, ALU.is_gt, ALU.add,
                                  accum_out=nover[:, :]).then_inc(s_k, 1)
                dve.tensor_scalar(ties[:, :], askT[:, :], th, None, ALU.is_equal, ALU.add,
                                  accum_out=nties[:, :]).then_inc(s_k, 1)
                dve.wait_ge(s_k, 3)
                dve.tensor_tensor_scan(order[:, :], ties[:, :], ties[:, :], 0.0, ALU.add, ALU.bypass).then_inc(s_k, 1)
                dve.wait_ge(s_su, ROUNDS + 1)
                dve.tensor_scalar(room[:, :], pC[0:R, 0:1], -1.0, float(CAP), ALU.mult, ALU.add).then_inc(s_k, 1)
                dve.wait_ge(s_k, 5)
                dve.scalar_tensor_tensor(out=kept[:, :], in0=order[:, :], scalar=room[:, 0:1], in1=ties[:, :],
                                         op0=ALU.is_le, op1=ALU.mult).then_inc(s_k, 1)
                dve.wait_ge(s_k, 6)
                dve.tensor_tensor(kept[:, :], kept[:, :], over[:, :], ALU.add).then_inc(s_ps, 1)
                dve.wait_ge(s_ps, ROUNDS + 1)
                dve.scalar_tensor_tensor(out=kept[:, :], in0=kept[:, :], scalar=0.5, in1=askT[:, :],
                                         op0=ALU.mult, op1=ALU.mult).then_inc(s_k, 1)
                dve.memset(weight[:, :, 0:1], 0.5).then_inc(s_wt, 1)
                dve.wait_ge(s_kt, 1)
                dve.tensor_copy(weight[:, :, 1:EX], pL[:, 0:R].rearrange("p (t e) -> p t e", e=ER)).then_inc(s_wt, 1)
                dve.wait_ge(s_wt, 2)

                def hidden(n, k):
                    dve.wait_ge(s_si, n * UNITS + k + 1)
                    if not (isinstance(n, int) and n == 0 and k < 2):
                        dve.wait_ge(s_hT, n * UNITS + k - 1)
                    dve.tensor_tensor(hidden_f[:, k % 2, :], sil[:, k % 2, :], pH[k % 2][:, :], ALU.mult).then_inc(s_hf, 1)

                def add(n, k):
                    j, blk = (k % UNITS) // NBLK, k % NBLK
                    for t in range(TB):
                        if t % 2 == 0:
                            dve.wait_ge(s_o, (n * UNITS + k) * 2 + t // 2 + 1)
                        xt = x[:, blk * TB + t, :]
                        e = n * 2 + j - (2 if k < 0 else 0)
                        dve.scalar_tensor_tensor(out=xt, in0=pO[t // 2][:, (t % 2) * D:(t % 2 + 1) * D],
                                                 scalar=weight[:, blk * TB + t, bass.ds(e, 1)], in1=xt,
                                                 op0=ALU.mult, op1=ALU.add).then_inc(s_x, 1)

                def unit(n, k):
                    hidden(n, k)
                    if not (isinstance(n, int) and n == 0 and k == 0):
                        add(n, k - 1)

                steps(dve, unit, lambda n, j: None)
                add(EX // 2 - 1, UNITS - 1)


def attention(nc, stage, x, psum, consts, w):
    H, HKV, DH = 16, 4, 128
    HG = H // HKV
    QT = L // P
    SLOTS = HG * QT
    UNITS = SLOTS // TB
    LAG = 3
    PB = 4
    SCALE = float(DH) ** -0.5
    LOW = -1e30
    EVENTS = {1: ("q", 2, 0), 3: ("v", 0, 0), 5: ("q", 3, 0), 7: ("o", 2, -1), 9: ("k", 1, 0), 11: ("q", 4, 0),
              13: ("v", 1, 0), 15: ("q", 5, 0), 17: ("o", 3, -1), 19: ("q", 6, 0), 21: ("q", 7, 0),
              23: ("o", 0, 0), 25: ("k", 0, 1), 27: ("q", 0, 1), 29: ("q", 1, 1), 30: ("o", 1, 0)}
    ROPES = [e[0:2] for e in EVENTS.values() if e[0] in "qk"]
    START = [("k", 0), ("q", 0), ("q", 1)]
    NR = len(ROPES)
    CUTS = {}
    for slot, (what, which, ahead) in EVENTS.items():
        if what in "qk":
            at = slot + 2 if what == "k" else max(slot + 2, TB * (which + UNITS * ahead) - TB - 1)
            CUTS[at] = (what, which, ahead)
    WK_AT, WQ_AT, WO_AT = 10, 22, 18
    with ExitStack() as ctx:
        pool = Pools(nc, ctx, stage, FIRST_STAGE_SEM)
        prob = pool.sb("prob", [P, PB, L])
        xT = Split(pool, "xT", [P, KD, N])
        norm = NormAll(pool, x, psum, consts, prob, xT)
        raw_gate, wgate = pool.sb("gate_w", [P, KD, 2 * H]), Split(pool, "gate_w", [P, KD, 2 * H])
        logits = Logits(pool, psum, consts, norm, wgate, 2 * H,
                        prob[0:2 * H, 2:4, :].rearrange("p a b -> p (a b)"))
        raw_q, wq = pool.sb("wq", [P, KD, HG * DH]), Split(pool, "wq", [P, KD, HG * DH])
        raw_k, wk = pool.sb("wk", [P, KD, DH]), Split(pool, "wk", [P, KD, DH])
        raw_v, wv = pool.sb("wv", [P, KD, DH]), Split(pool, "wv", [P, KD, DH])
        raw_o, wo = pool.sb("wo", [P, HG, D]), Split(pool, "wo", [P, HG, D])
        cos, sin = pool.sb("cos", [P, L]), pool.sb("sin", [P, L])
        later = pool.sb("later_keys", [P, P], BF16)
        both = pool.sb("both_gates", [P, NT, 2 * H])
        gate = pool.sb("gate", [P, NT, H])
        step_gate = pool.sb("step_gate", [P, NB, QT, HG])
        k0, k1 = Split(pool, "k_first", [P, NB, BLK]), Split(pool, "k_second", [P, BLK])
        v = Split(pool, "v", [P, QT, DH])
        q = Split(pool, "q", [P, 2, BLK])
        straight, swapped = pool.sb("rope_straight", [P, BLK]), pool.sb("rope_swapped", [P, BLK])
        roped = pool.sb("roped", [P, BLK])
        top = pool.sb("row_max", [P, SLOTS])
        ntop = pool.sb("minus_max", [P, SLOTS])
        den = pool.sb("row_sum", [P, SLOTS])
        rden = pool.sb("inv_row_sum", [P, SLOTS])
        pT = Split(pool, "probT", [P, QT, BLK])
        oT = Split(pool, "headsT", [P, 2, HG, BLK])

        s_tab = pool.sem("tables_loaded")
        s_lt = pool.sem("later_built")
        s_gw, s_gh = pool.sem("gate_w_loaded"), pool.sem("gate_w_hi")
        s_gc = pool.sem("step_gates")
        s_gs = pool.sem("gates_squashed")
        s_gt = pool.sem("gates_ready")
        s_ld = {n: pool.sem(f"{n}_loaded") for n in ("wq", "wk", "wv", "wo")}
        s_wh = {n: pool.sem(f"{n}_hi") for n in ("wq", "wk", "wv", "wo")}
        s_wl = {n: pool.sem(f"{n}_lo") for n in ("wq", "wk", "wv", "wo")}
        weights = {"wq": (raw_q, wq), "wk": (raw_k, wk), "wv": (raw_v, wv), "wo": (raw_o, wo)}
        s_pj = pool.sem("projected")
        s_rs = pool.sem("rope_straight")
        s_rw = pool.sem("rope_swapped")
        s_rc = pool.sem("rope_cos")
        s_rd = pool.sem("roped")
        s_rh = pool.sem("rope_hi")
        s_rl = pool.sem("rope_lo")
        s_vp = pool.sem("v_projected")
        s_vh, s_vl = pool.sem("v_hi"), pool.sem("v_lo")
        s_sc = pool.sem("scores")
        s_mx = pool.sem("max_ready")
        s_nb = pool.sem("minus_max_ready")
        s_ex = pool.sem("exp_done")
        s_ri = pool.sem("inv_sum_ready")
        s_sp = pool.sem("prob_scaled")
        s_tr = pool.sem("prob_turned")
        s_ph, s_pl = pool.sem("probT_hi"), pool.sem("probT_lo")
        s_pv = pool.sem("pv_done")
        s_oh, s_ol = pool.sem("headsT_hi"), pool.sem("headsT_lo")
        s_op = pool.sem("out_products")
        s_xa = pool.sem("residual_added")
        mark = pool.sem("mark")
        score = [psum.pair(0).rearrange("p a b -> p (a b)"), psum.pair(2).rearrange("p a b -> p (a b)")]
        turn = psum[4:6]
        pv_bank, bank = psum[6], psum[7]

        def prime(eng, *sems):
            for s, per in sems:
                eng.sem_inc(s, per)

        def steps(eng, step, tail):
            for b in range(NB):
                step(1 + b, b, 0, b == 0, False)
            with eng.Fori(1, HKV - 1) as hk:
                for b in range(NB):
                    step(hk * NB + 1 + b, b, hk, False, False)
            for b in range(NB):
                step((HKV - 1) * NB + 1 + b, b, HKV - 1, False, b == NB - 1)
            tail((HKV - 1) * NB + NB, NB - 1, HKV - 1)

        def slot_events(s, first, last):
            e = EVENTS.get(s)
            if e and not (first and e[2] < 0) and not (last and e[2] > 0):
                return e
            return None

        def seq(b, ahead):
            return (b + ahead) % NB

        def rope_count(g, what, which):
            early = (what, which) in START
            return (g - early) * NR + ROPES.index((what, which)) + 1

        def start_count(i):
            return NR - len(START) + i + 1

        def tile(n):
            u = n // TB
            return u, u % HG, u // HG, u // HG * TB + n % TB

        def parts(n):
            u, h, c, i = tile(n)
            if c == 0:
                return [(n, 0, i + 1)]
            first = SLOTS // 2 + 2 * (n - SLOTS // 2)
            return [(first, 0, TB), (first + 1, TB, i + 1 - TB)]

        def through(g, n):
            return (g - (n < 0)) * NP + parts(n % SLOTS)[-1][0] + 1

        NP = SLOTS // 2 * 3
        order = sorted(EVENTS)

        with nc.Block() as block:
            @block.sync
            def _(sp):
                sp.dma_start(raw_gate[:, :, :], w["gate_w"].rearrange("(k p) e -> p k e", p=P)).then_inc(s_gw, 16)

                def load(h, cut):
                    for n, per in (("wk", DH), ("wq", HG * DH), ("wv", DH), ("wo", HG * DH)):
                        if cut is not None:
                            sp.wait_ge(s_wl[n], cut)
                        raw = weights[n][0]
                        if n == "wo":
                            src = w[n][bass.ds(h * per, per), :].rearrange("(h p) d -> p h d", p=P)
                        else:
                            src = w[n].rearrange("(k p) f -> p k f", p=P)[:, :, bass.ds(h * per, per)]
                        sp.dma_start(raw[:, :, :], src).then_inc(s_ld[n], 16)

                load(0, None)
                sp.dma_start(cos[:, :], w["cos"]).then_inc(s_tab, 16)
                sp.dma_start(sin[:, :], w["sin"]).then_inc(s_tab, 16)
                with sp.Fori(1, HKV) as h:
                    load(h, h)

            def act_cut_weight(act, n, hk):
                raw, wt = weights[n]
                act.wait_ge(s_ld[n], hk * 16 + 16)
                act.copy(wt.hi[:, :, :], raw[:, :, :]).then_inc(s_wh[n], 1)

            def pool_cut_weight(pl, n, hk):
                raw, wt = weights[n]
                pl.wait_ge(s_wh[n], hk + 1)
                take_rest(pl, wt.lo[:, :, :], raw[:, :, :], wt.hi[:, :, :]).then_inc(s_wl[n], 1)

            @block.gpsimd
            def _(pl):
                pl.memset(later[:, :], 0.0).then_inc(s_lt, 1)
                pl.wait_ge(s_lt, 1)
                pl.affine_select(out=later[:, :], in_=later[:, :], pattern=[[-1, P]], compare_op=ALU.is_ge, fill=LOW,
                                 base=0, channel_multiplier=1).then_inc(s_lt, 1)
                pl.wait_ge(s_gh, 1)
                take_rest(pl, wgate.lo[:, :, :], raw_gate[:, :, :], wgate.hi[:, :, :]).then_inc(logits.s_w, 1)
                for n in ("wk", "wq", "wv", "wo"):
                    pool_cut_weight(pl, n, 0)
                prime(pl, (s_rc, NR - len(START)), (s_rd, NR - len(START)), (s_rl, NR - len(START)), (s_sp, SLOTS))

                def rope_cos(m, what, which):
                    c = which if what == "k" else which // HG
                    cols = slice(c * BLK, (c + 1) * BLK)
                    pl.wait_ge(s_rs, m)
                    pl.wait_ge(s_rl, m - 1)
                    pl.tensor_tensor(roped[:, :], straight[:, :], cos[:, cols], ALU.mult).then_inc(s_rc, 1)

                def rope_add(m):
                    pl.wait_ge(s_rc, m)
                    pl.wait_ge(s_rw, 2 * m)
                    pl.tensor_tensor(roped[:, :], roped[:, :], swapped[:, :], ALU.add).then_inc(s_rd, 1)

                def cut(m, b, what, which):
                    pl.wait_ge(s_rh, m)
                    dst = q[:, which % 2, :] if what == "q" else (k0[:, b, :], k1[:, :])[which]
                    take_rest(pl, dst[1], roped[:, :], dst[0]).then_inc(s_rl, 1)

                def scale(g, b, n):
                    u, h, c, i = tile(n)
                    pl.wait_ge(s_ri, g * SLOTS + n + 1)
                    alone(pl, mark)
                    pr = prob[:, n % PB, 0:(i + 1) * P]
                    pl.tensor_scalar(pr, pr, rden[:, n:n + 1], step_gate[:, b, i, h:h + 1],
                                     ALU.mult, ALU.mult).then_inc(s_sp, 1)

                pl.wait_ge(s_tab, 32)
                pl.wait_ge(s_gt, 1)
                for i, (what, which) in enumerate(START):
                    rope_cos(start_count(i), what, which)
                    rope_add(start_count(i))
                    cut(start_count(i), 0, what, which)

                def step(g, b, hk, first, last):
                    for s in range(SLOTS):
                        if s >= 1:
                            scale(g, b, s - 1)
                        elif not first:
                            scale(g - 1, seq(b, -1), SLOTS - 1)
                        if s == 0:
                            pl.tensor_copy(step_gate[:, b, :, :], gate[:, b * QT:(b + 1) * QT, bass.ds(hk * HG, HG)]).then_inc(s_gc, 1)
                            pl.wait_ge(s_gc, g)
                        if s == WK_AT and b == NB - 1 and not last:
                            pool_cut_weight(pl, "wk", hk + 1)
                        if s == WQ_AT and b == NB - 1 and not last:
                            pool_cut_weight(pl, "wq", hk + 1)
                            pool_cut_weight(pl, "wv", hk + 1)
                        if s == WO_AT and b == 0 and not first:
                            pool_cut_weight(pl, "wo", hk)
                        if s in CUTS and not (last and CUTS[s][2]):
                            what, which, ahead = CUTS[s]
                            cut(rope_count(g + ahead, what, which), seq(b, ahead), what, which)
                        e = slot_events(s - 1, first, last)
                        if e and e[0] in "qk":
                            rope_add(rope_count(g + e[2], e[0], e[1]))
                        e = slot_events(s, first, last)
                        if e and e[0] in "qk":
                            rope_cos(rope_count(g + e[2], e[0], e[1]), e[0], e[1])

                steps(pl, step, lambda g, b, hk: scale(g, b, SLOTS - 1))

            @block.tensor
            def _(pe):
                norm.pe(pe, logits)
                logits.pe_turn(pe)
                norm.wait(pe)
                prime(pe, (s_pj, NR - len(START)), (s_vp, 2), (s_sc, SLOTS), (s_tr, NP), (s_pv, 2 * UNITS), (s_op, 4))
                pe.wait_ge(s_lt, 2)
                pe.wait_ge(s_gs, 1)

                def bank_free(g, s, first, last):
                    before = [EVENTS[t] for t in order if t < s and slot_events(t, first, last)]
                    if before:
                        what, which, ahead = before[-1]
                    elif first:
                        what, which, ahead = START[-1] + (0,)
                    else:
                        what, which, ahead = EVENTS[order[-1]]
                        ahead -= 1
                    if what == "v":
                        pe.wait_ge(s_vh, (g + ahead) * 2 + which + 1)
                        pe.wait_ge(s_vl, (g + ahead) * 2 + which + 1)
                    elif what == "o":
                        pe.wait_ge(s_xa, (g + ahead) * 4 + which + 1)
                    else:
                        pe.wait_ge(s_rs, rope_count(g + ahead, what, which))

                def project(b, what, which, wsem, hk):
                    c, head = (which, 0) if what == "k" else (which // HG, which % HG)
                    wt = wk if what == "k" else wq
                    pe.wait_ge(s_wl[wsem], hk + 1)
                    for k in range(KD):
                        ins = matmul_split(pe, bank[:, :], wt[:, k, head * DH:(head + 1) * DH],
                                           xT[:, k, b * L + c * BLK:b * L + (c + 1) * BLK], k == 0, k == KD - 1)
                    ins.then_inc(s_pj, 1)

                def project_v(b, c, hk):
                    pe.wait_ge(s_wl["wv"], hk + 1)
                    for t in range(TB):
                        r = b * L + (c * TB + t) * P
                        for k in range(KD):
                            ins = matmul_split(pe, bank[:, t * P:(t + 1) * P], xT[:, k, r:r + P], wv[:, k, :],
                                               k == 0, k == KD - 1)
                    ins.then_inc(s_vp, 1)

                def outputs(g, quarter, hk):
                    c = quarter // 2
                    pe.wait_ge(s_wl["wo"], hk + 1)
                    pe.wait_ge(s_ol, g * UNITS + HG * (c + 1))
                    for t in range(2):
                        cols = slice((quarter % 2 * 2 + t) * P, (quarter % 2 * 2 + t + 1) * P)
                        for h in range(HG):
                            ins = matmul_split(pe, bank[:, t * D:(t + 1) * D], oT[:, c, h, cols], wo[:, h, :],
                                               h == 0, h == HG - 1)
                    ins.then_inc(s_op, 1)

                def scores(g, b, n):
                    u, h, c, i = tile(n)
                    if n % TB == 0:
                        pe.wait_ge(s_rl, rope_count(g, "q", u))
                    if n == HG * TB:
                        pe.wait_ge(s_rl, rope_count(g, "k", 1))
                    pe.wait_ge(s_ex, g * SLOTS + n - 1)
                    dst = score[n % 2]
                    lhs = q[:, u % 2, i % TB * P:(i % TB + 1) * P]
                    for kb in range(c + 1):
                        width = min(BLK, (i + 1) * P - kb * BLK)
                        keys = k0[:, b, 0:width] if kb == 0 else k1[:, 0:width]
                        matmul_split(pe, dst[:, kb * BLK:kb * BLK + width], lhs, keys, True, kb < c)
                    pe.matmul(dst[:, i * P:(i + 1) * P], consts["ident_bf"][:, :], later[:, :],
                              start=False, stop=True).then_inc(s_sc, 1)

                def turn_tile(g, n):
                    u, h, c, i = tile(n)
                    pe.wait_ge(s_sp, g * SLOTS + n + 1)
                    for part, lo, width in parts(n):
                        pe.wait_ge(s_pl, g * NP + part - 1)
                        for j in range(width):
                            ins = pe.transpose(turn[part % 2][:, j * P:(j + 1) * P],
                                               prob[:, n % PB, (lo + j) * P:(lo + j + 1) * P], consts["ident"][:, :])
                        ins.then_inc(s_tr, 1)

                def pv(g, u, half):
                    c = u // HG
                    pe.wait_ge(s_pl, through(g, TB * u + 2 * half + 1))
                    if u % HG == 0 and half == 0:
                        pe.wait_ge(s_vl, g * 2 + c + 1)
                    pe.wait_ge(s_ol, g * UNITS + u)
                    first, end = 2 * half * P, 2 * (half + 1) * P
                    last_key = TB * c + 2 * half + 1
                    for j in range(last_key + 1):
                        lo = max(first, (j - TB * c) * P)
                        ins = matmul_split(pe, pv_bank[:, lo:end], v[:, j, :], pT[:, j, lo:end], j == 0, j == last_key)
                    ins.then_inc(s_pv, 1)

                for i, (what, which) in enumerate(START):
                    if i:
                        pe.wait_ge(s_rs, start_count(i - 1))
                    project(0, what, which, "wk" if what == "k" else "wq", 0)

                def step(g, b, hk, first, last):
                    for s in range(SLOTS):
                        scores(g, b, s)
                        e = slot_events(s, first, last)
                        if e:
                            what, which, ahead = e
                            bank_free(g, s, first, last)
                            bb = seq(b, ahead)
                            hh = hk if 0 <= b + ahead < NB else hk + ahead
                            if what == "o":
                                outputs(g + ahead, which, hh)
                            elif what == "v":
                                project_v(bb, which, hh)
                            else:
                                project(bb, what, which, "wk" if what == "k" else "wq", hh)
                        if s >= LAG:
                            turn_tile(g, s - LAG)
                        elif not first:
                            turn_tile(g - 1, s - LAG + SLOTS)
                        if s % 2:
                            if s > TB:
                                pv(g, s // TB - 1, s % TB // 2)
                            elif not first:
                                pv(g - 1, UNITS - 1, s % TB // 2)

                def tail(g, b, hk):
                    for n in range(SLOTS - LAG, SLOTS):
                        turn_tile(g, n)
                    pv(g, UNITS - 1, 0)
                    pv(g, UNITS - 1, 1)
                    outputs(g, 2, hk)
                    pe.wait_ge(s_xa, g * 4 + 3)
                    outputs(g, 3, hk)

                steps(pe, step, tail)

            @block.scalar
            def _(act):
                act.wait_ge(s_gw, 16)
                act.copy(wgate.hi[:, :, :], raw_gate[:, :, :]).then_inc(s_gh, 1)
                norm.act(act, logits)
                for n in ("wk", "wq", "wv", "wo"):
                    act_cut_weight(act, n, 0)
                act.wait_ge(logits.s_t, 1)
                act.activation(both[:, :, :], psum[4].rearrange("p (t g) -> p t g", t=NT), ACT.Sigmoid).then_inc(s_gs, 1)
                prime(act, (s_rs, NR - len(START)), (s_rh, NR - len(START)), (s_vh, 2), (s_ex, SLOTS), (s_ph, NP), (s_oh, UNITS))

                def straight_copy(m):
                    act.wait_ge(s_pj, m)
                    act.wait_ge(s_rc, m - 1)
                    act.wait_ge(s_rw, 2 * m - 2)
                    act.copy(straight[:, :], bank[:, :]).then_inc(s_rs, 1)

                def cut(g, b, what, which, m):
                    act.wait_ge(s_rd, m)
                    if what == "q":
                        act.wait_ge(s_sc, g * SLOTS + TB * (which - 1))
                        dst = q.hi[:, which % 2, :]
                    elif which == 0:
                        act.wait_ge(s_sc, (g - 1) * SLOTS)
                        dst = k0.hi[:, b, :]
                    else:
                        act.wait_ge(s_sc, g * SLOTS)
                        dst = k1.hi[:, :]
                    act.copy(dst, roped[:, :]).then_inc(s_rh, 1)

                def v_hi(g, c):
                    act.wait_ge(s_vp, g * 2 + c + 1)
                    act.wait_ge(s_pv, g * 2 * UNITS)
                    act.copy(v.hi[:, c * TB:(c + 1) * TB, :].rearrange("p t d -> p (t d)"), bank[:, :]).then_inc(s_vh, 1)

                def exps(g, n):
                    u, h, c, i = tile(n)
                    act.wait_ge(s_nb, g * SLOTS + n + 1)
                    act.wait_ge(s_tr, through(g, n - PB))
                    act.activation(prob[:, n % PB, 0:(i + 1) * P], score[n % 2][:, 0:(i + 1) * P], ACT.Exp,
                                   bias=ntop[:, n:n + 1], scale=SCALE, accum_out=den[:, n:n + 1]).then_inc(s_ex, 1)

                def prob_hi(g, n):
                    u, h, c, i = tile(n)
                    act.wait_ge(s_pv, (g * UNITS + u) * 2 - 1 + n % TB // 2)
                    for part, lo, width in parts(n):
                        act.wait_ge(s_tr, g * NP + part + 1)
                        act.copy(pT.hi[:, lo:lo + width, i % TB * P:(i % TB + 1) * P],
                                 turn[part % 2][:, 0:width * P].rearrange("p (j q) -> p j q", j=width)).then_inc(s_ph, 1)

                def head_hi(g, u):
                    c, h = u // HG, u % HG
                    act.wait_ge(s_pv, (g * UNITS + u + 1) * 2)
                    act.wait_ge(s_op, g * 4 - 2 + 2 * c)
                    act.copy(oT.hi[:, c, h, :], pv_bank[:, :]).then_inc(s_oh, 1)

                for i, (what, which) in enumerate(START):
                    straight_copy(start_count(i))
                    cut(1, 0, what, which, start_count(i))

                def step(g, b, hk, first, last):
                    for s in range(SLOTS):
                        e = slot_events(s, first, last)
                        if e and e[0] in "qk":
                            straight_copy(rope_count(g + e[2], e[0], e[1]))
                        if s >= LAG:
                            prob_hi(g, s - LAG)
                        elif not first:
                            prob_hi(g - 1, s - LAG + SLOTS)
                        exps(g, s)
                        if s % TB == TB - 1:
                            if s >= 2 * TB - 1:
                                head_hi(g, s // TB - 1)
                            elif not first:
                                head_hi(g - 1, UNITS - 1)
                        if e and e[0] == "v":
                            v_hi(g, e[1])
                        if s in CUTS and not (last and CUTS[s][2]):
                            what, which, ahead = CUTS[s]
                            cut(g + ahead, seq(b, ahead), what, which, rope_count(g + ahead, what, which))
                        if s == WK_AT and b == NB - 1 and not last:
                            act.wait_ge(s_pj, rope_count(g, "k", 1))
                            act_cut_weight(act, "wk", hk + 1)
                        if s == WQ_AT and b == NB - 1 and not last:
                            act.wait_ge(s_pj, rope_count(g, "q", UNITS - 1))
                            act.wait_ge(s_vp, g * 2 + 2)
                            act_cut_weight(act, "wq", hk + 1)
                            act_cut_weight(act, "wv", hk + 1)
                        if s == WO_AT and b == 0 and not first:
                            act.wait_ge(s_op, g * 4)
                            act_cut_weight(act, "wo", hk)

                def tail(g, b, hk):
                    for n in range(SLOTS - LAG, SLOTS):
                        prob_hi(g, n)
                    head_hi(g, UNITS - 1)

                steps(act, step, tail)

            @block.vector
            def _(dve):
                norm.dve(dve)
                dve.wait_ge(s_gs, 1)
                dve.tensor_tensor(gate[:, :, :], both[:, :, 0:H], both[:, :, H:2 * H], ALU.add).then_inc(s_gt, 1)
                dve.wait_ge(s_tab, 32)
                prime(dve, (s_rw, 2 * (NR - len(START))), (s_vl, 2), (s_mx, SLOTS), (s_nb, SLOTS), (s_ri, SLOTS), (s_pl, NP),
                      (s_ol, UNITS), (s_xa, 4))

                def swap(m, what, which):
                    c = which if what == "k" else which // HG
                    cols = slice(c * BLK, (c + 1) * BLK)
                    half = P // 2
                    dve.wait_ge(s_rs, m)
                    dve.wait_ge(s_rd, m - 1)
                    dve.tensor_tensor(swapped[0:half, :], straight[half:P, :], sin[half:P, cols], ALU.mult).then_inc(s_rw, 1)
                    dve.tensor_tensor(swapped[half:P, :], straight[0:half, :], sin[0:half, cols], ALU.mult).then_inc(s_rw, 1)

                def v_lo(g, c):
                    dve.wait_ge(s_vh, g * 2 + c + 1)
                    at = slice(c * TB, (c + 1) * TB)
                    take_rest(dve, v.lo[:, at, :].rearrange("p t d -> p (t d)"), bank[:, :],
                              v.hi[:, at, :].rearrange("p t d -> p (t d)")).then_inc(s_vl, 1)

                def maxima(g, n):
                    u, h, c, i = tile(n)
                    dve.wait_ge(s_sc, g * SLOTS + n + 1)
                    dve.tensor_reduce(top[:, n:n + 1], score[n % 2][:, 0:(i + 1) * P], AX.X, ALU.max).then_inc(s_mx, 1)
                    dve.wait_ge(s_mx, g * SLOTS + n + 1)
                    dve.tensor_scalar(ntop[:, n:n + 1], top[:, n:n + 1], -SCALE, None, ALU.mult).then_inc(s_nb, 1)

                def inv_sum(g, n):
                    dve.wait_ge(s_ex, g * SLOTS + n + 1)
                    dve.wait_ge(s_sp, (g - 1) * SLOTS + n + 1)
                    dve.reciprocal(rden[:, n:n + 1], den[:, n:n + 1]).then_inc(s_ri, 1)

                def prob_lo(g, n):
                    u, h, c, i = tile(n)
                    cols = slice(i % TB * P, (i % TB + 1) * P)
                    for part, lo, width in parts(n):
                        dve.wait_ge(s_ph, g * NP + part + 1)
                        take_rest(dve, pT.lo[:, lo:lo + width, cols],
                                  turn[part % 2][:, 0:width * P].rearrange("p (j q) -> p j q", j=width),
                                  pT.hi[:, lo:lo + width, cols]).then_inc(s_pl, 1)

                def head_lo(g, u):
                    c, h = u // HG, u % HG
                    dve.wait_ge(s_oh, g * UNITS + u + 1)
                    take_rest(dve, oT.lo[:, c, h, :], pv_bank[:, :], oT.hi[:, c, h, :]).then_inc(s_ol, 1)

                def residual(g, b, quarter):
                    dve.wait_ge(s_op, g * 4 + quarter + 1)
                    xt = x[:, b * QT + 2 * quarter:b * QT + 2 * quarter + 2, :]
                    dve.tensor_tensor(xt, xt, bank.rearrange("p (t d) -> p t d", t=2), ALU.add).then_inc(s_xa, 1)

                for i, (what, which) in enumerate(START):
                    swap(start_count(i), what, which)

                def step(g, b, hk, first, last):
                    for s in range(SLOTS):
                        maxima(g, s)
                        e = slot_events(s - 1, first, last)
                        if e and e[0] in "qk":
                            swap(rope_count(g + e[2], e[0], e[1]), e[0], e[1])
                        e = slot_events(s, first, last)
                        if e and e[0] == "o":
                            residual(g + e[2], seq(b, e[2]), e[1])
                        if s >= 1:
                            inv_sum(g, s - 1)
                        elif not first:
                            inv_sum(g - 1, SLOTS - 1)
                        if s >= LAG:
                            prob_lo(g, s - LAG)
                        elif not first:
                            prob_lo(g - 1, s - LAG + SLOTS)
                        if s % TB == TB - 1:
                            if s >= 2 * TB - 1:
                                head_lo(g, s // TB - 1)
                            elif not first:
                                head_lo(g - 1, UNITS - 1)
                        if e and e[0] == "v":
                            v_lo(g, e[1])

                def tail(g, b, hk):
                    inv_sum(g, SLOTS - 1)
                    for n in range(SLOTS - LAG, SLOTS):
                        prob_lo(g, n)
                    head_lo(g, UNITS - 1)
                    residual(g, b, 2)
                    residual(g, b, 3)

                steps(dve, step, tail)


def mamba(nc, stage, x, psum, consts, w):
    DI, S, TAPS, DTR = 512, 16, 4, 16
    C = DI // P
    NCH = L // BLK
    CHS = NB * NCH
    G = 4
    STEPS = S // G
    U = G * C
    ROWS = 2 * S + DTR
    with ExitStack() as ctx:
        pool = Pools(nc, ctx, stage, FIRST_STAGE_SEM)
        xT = pool.sb("xT", [P, KD, N])
        win = pool.sb("in_proj_w", [P, KD, 2 * DI])
        wx = pool.sb("x_proj_w", [P, C, ROWS])
        wdt = pool.sb("dt_proj_w_and_bias", [DTR + 1, DI])
        wout = pool.sb("out_proj_w", [P, C, D])
        cw, cb = pool.sb("conv_w", [P, C, TAPS]), pool.sb("conv_b", [P, C])
        skip = pool.sb("D", [P, C])
        skipd = pool.sb("D_diagonal", [P, C, P])
        a = pool.sb("A", [P, C, S])
        pick = pool.sb("row_to_all", [6 * S, 2 * S, P], BF16)
        xpad = pool.sb("x_with_history", [P, C, BLK + TAPS - 1])
        conv = pool.sb("conv", [P, 2, BLK])
        xc = pool.sb("x_conv", [P, C, BLK])
        sz = pool.sb("silu_z", [P, C, BLK])
        dtl = pool.sb("dt_low", [DTR + 1, BLK])
        bc3 = pool.sb("BC_parts", [6 * S, BLK], BF16)
        left = pool.sb("BC_left", [2 * S, BLK])
        mid = pool.sb("BC_mid", [2 * S, BLK], BF16)
        e = pool.sb("exp_minus_abs", [P, C * BLK])
        u = pool.sb("one_plus_exp", [P, C * BLK])
        pos = pool.sb("positive_part", [P, C * BLK])
        delta = pool.sb("delta", [P, C * BLK])
        dx = pool.sb("delta_x", [P, C * BLK])
        inp = pool.sb("state_input", [P, 4, BLK])
        h = pool.sb("state", [P, 4, BLK])
        hc = pool.sb("state_times_C", [P, 4, BLK])
        call = pool.sb("C_on_all", [P, 2, BLK])
        last = pool.sb("last_state", [P, C, S])
        ys = pool.sb("y_gated", [P, C, BLK])

        norm = NormAll(pool, x, psum, consts, e[:, :].rearrange("p (i c) -> p i c", i=2), xT)
        s_w = pool.sem("weights_loaded")
        s_pk = pool.sem("row_pick_built")
        s_a = pool.sem("A_ready")
        s_in = pool.sem("setup_done")
        s_xp, s_zp = pool.sem("x_projected"), pool.sem("z_projected")
        s_xe, s_ze = pool.sem("x_in_sbuf"), pool.sem("silu_z_ready")
        s_cs, s_cv = pool.sem("conv_step"), pool.sem("conv_ready")
        s_xc, s_cr = pool.sem("x_conv_ready"), pool.sem("history_kept")
        s_xd, s_dl = pool.sem("x_dbl_products"), pool.sem("dt_low_ready")
        s_bs, s_b3, s_md = pool.sem("BC_step"), pool.sem("BC_parts_ready"), pool.sem("BC_mid_ready")
        s_dp, s_ab, s_e = pool.sem("dt_products"), pool.sem("abs_done"), pool.sem("exp_done")
        s_ps, s_u, s_ln, s_de = pool.sem("positive_ready"), pool.sem("u_ready"), pool.sem("log_ready"), pool.sem("delta_step")
        s_dx = pool.sem("delta_x_ready")
        s_yi = pool.sem("skip_product")
        s_B, s_C, s_Cs = pool.sem("B_on_all"), pool.sem("C_on_all"), pool.sem("C_in_sbuf")
        s_dA, s_db, s_h = pool.sem("decay_ready"), pool.sem("input_ready"), pool.sem("state_ready")
        s_hl, s_hc, s_y = pool.sem("last_state_kept"), pool.sem("state_C_ready"), pool.sem("y_summed")
        s_ys, s_op, s_xa = pool.sem("y_gated"), pool.sem("out_products"), pool.sem("residual_added")
        s_z = pool.sem("last_state_cleared")
        mark = pool.sem("mark")
        NW = 8
        bankB, bankC, bankA, bankY = psum[0], psum[1], psum[2:4], psum[4:8]
        bankO = psum[6:8]
        bankX, bankZ = psum[0:4], psum[1:4] + psum[0:1]
        dt_banks = psum.whole[:, 4:8, :].rearrange("p c t -> p (c t)")

        with nc.Block() as block:
            @block.sync
            def _(sp):
                for dst, src in ((win[:, :, :], w["in_proj_w"].rearrange("(k p) e -> p k e", p=P)),
                                 (wx[:, :, :], w["x_proj_w"].rearrange("(c p) r -> p c r", p=P)),
                                 (wdt[:, :], w["dt_proj_w"]),
                                 (wout[:, :, :], w["out_proj_w"].rearrange("(c p) d -> p c d", p=P)),
                                 (cw[:, :, :], w["conv_w"].rearrange("(c p) k -> p c k", p=P)),
                                 (cb[:, :], w["conv_b"]),
                                 (skip[:, :], w["D"]),
                                 (a[:, :, :], w["A_log"].rearrange("(c p) s -> p c s", p=P))):
                    sp.dma_start(dst, src).then_inc(s_w, 16)

            @block.gpsimd
            def _(pl):
                pl.memset(pick[:, :, :], 0.0).then_inc(s_pk, 1)
                for part in range(3):
                    pl.wait_ge(s_pk, part + 1)
                    pl.affine_select(out=pick[:, :, :], in_=pick[:, :, :], pattern=[[-1, 2 * S], [0, P]],
                                     compare_op=ALU.not_equal, fill=1.0, base=-2 * S * part,
                                     channel_multiplier=1).then_inc(s_pk, 1)
                pl.sem_inc(s_hc, U)
                with pl.Fori(0, CHS * STEPS) as step:
                    q = step + 1
                    for j in range(U):
                        pl.wait_ge(s_h, q * U + j + 1)
                        if j % C == 0:
                            pl.wait_ge(s_Cs, q * G + j // C + 1)
                        pl.wait_ge(s_y, q * U + j - 3)
                        pl.tensor_tensor(hc[:, j % 4, :], h[:, j % 4, :], call[:, j // C % 2, :],
                                         ALU.mult).then_inc(s_hc, 1)

            @block.tensor
            def _(pe):
                norm.pe(pe)
                norm.wait(pe)
                pe.wait_ge(s_w, NW * 16)
                for s, per in ((s_B, G), (s_C, G), (s_y, U)):
                    pe.sem_inc(s, per)

                def ysum(q, j):
                    pe.wait_ge(s_hc, q * U + j + 1)
                    pe.matmul(bankY[j % C][:, :], consts["ident"][:, :], hc[:, j % 4, :], start=False, stop=True,
                              skip_group_check=True).then_inc(s_y, 1)

                def states(ch, pp, first):
                    q = ch * STEPS + pp + 1
                    for j in range(G):
                        n = pp * G + j
                        if first and j == 0:
                            pe.wait_ge(s_b3, ch + 1)
                            pe.wait_ge(s_md, ch + 1)
                            pe.wait_ge(s_dl, ch + 1)
                        pe.wait_ge(s_db, q * U + j * C)
                        alone(pe, mark)
                        pe.matmul(bankB[:, :], pick[:, bass.ds(n, 1), :].rearrange("r a p -> r (a p)"), bc3[:, :],
                                  start=True, stop=True).then_inc(s_B, 1)
                        pe.wait_ge(s_Cs, q * G + j)
                        alone(pe, mark)
                        pe.matmul(bankC[:, :], pick[:, bass.ds(n + S, 1), :].rearrange("r a p -> r (a p)"), bc3[:, :],
                                  start=True, stop=True).then_inc(s_C, 1)
                        if not (first and j == 0):
                            for c in range(C):
                                ysum(q, (j - 1) * C + c)

                def project(ch, half, banks, done):
                    for c in range(C):
                        if half == 1 and c == C - 1:
                            pe.wait_ge(s_dl, ch + 1)
                            pe.wait_ge(s_b3, ch + 1)
                        for k in range(KD):
                            ins = pe.matmul(banks[c][:, :], win[:, k, half * DI + c * P:half * DI + (c + 1) * P],
                                            xT[:, k, ch * BLK:(ch + 1) * BLK], start=(k == 0), stop=(k == KD - 1))
                        ins.then_inc(done, 1)

                project(0, 0, bankX, s_xp)
                for ch in range(CHS):
                    pe.wait_ge(s_xe, ch * C + C)
                    for c in range(C):
                        pe.wait_ge(s_xc, ch * C + c + 1)
                        ins = pe.matmul(psum[0][0:ROWS, :], wx[:, c, :], xc[:, c, :], start=(c == 0), stop=(c == C - 1))
                    ins.then_inc(s_xd, 1)
                    pe.wait_ge(s_dl, ch + 1)
                    if ch > 0:
                        pe.wait_ge(s_xa, ch * 2 + 2)
                    for c in range(C):
                        ins = pe.matmul(bankY[c][:, :], wdt[:, c * P:(c + 1) * P], dtl[:, :], start=True, stop=True)
                    ins.then_inc(s_dp, 1)
                    project(ch, 1, bankZ, s_zp)
                    pe.wait_ge(s_ab, ch + 1)
                    pe.wait_ge(s_ps, ch + 1)
                    if ch == 0:
                        pe.wait_ge(s_in, 1)
                        pe.wait_ge(s_pk, 4)
                    for c in range(C):
                        ins = pe.matmul(bankY[c][:, :], skipd[:, c, :], xc[:, c, :], start=True, stop=True,
                                        skip_group_check=True)
                    ins.then_inc(s_yi, 1)
                    pe.wait_ge(s_ze, ch * C + C)
                    states(ch, 0, True)
                    with pe.Fori(1, STEPS) as pp:
                        states(ch, pp, False)
                    for c in range(C):
                        ysum((ch + 1) * STEPS, (G - 1) * C + c)
                    if ch + 1 < CHS:
                        pe.wait_ge(s_h, ((ch + 1) * STEPS + 1) * U)
                        pe.wait_ge(s_Cs, ((ch + 1) * STEPS + 1) * G)
                        project(ch + 1, 0, bankX, s_xp)
                    pe.wait_ge(s_ys, ch * C + C)
                    for t in range(TB):
                        for c in range(C):
                            ins = pe.matmul(bankO[t // 2][:, (t % 2) * D:(t % 2 + 1) * D], ys[:, c, t * P:(t + 1) * P],
                                            wout[:, c, :], start=(c == 0), stop=(c == C - 1))
                        if t % 2:
                            ins.then_inc(s_op, 1)

            @block.scalar
            def _(act):
                norm.act(act)
                act.wait_ge(s_w, NW * 16)
                act.activation(a[:, :, :], a[:, :, :], ACT.Exp).then_inc(s_a, 1)
                BEHIND = 2

                def keep_last(ch, pp, i):
                    act.wait_ge(s_h, (ch * STEPS + pp + 1) * U + i + 1)
                    act.copy(last[:, i % C, bass.ds(pp * G + i // C, 1)], h[:, i % 4, BLK - 1:BLK]).then_inc(s_hl, 1)

                def decays(ch, pp, first):
                    q = ch * STEPS + pp + 1
                    for j in range(U):
                        if j % C == 0:
                            act.wait_ge(s_C, q * G + j // C + 1)
                            act.wait_ge(s_hc, q * U + (j // C - 1) * C)
                            act.copy(call[:, j // C % 2, :], bankC[:, :]).then_inc(s_Cs, 1)
                        act.wait_ge(s_h, q * U + j - 1)
                        c = j % C
                        act.activation(bankA[j % 2][:, :], delta[:, c * BLK:(c + 1) * BLK], ACT.Exp,
                                       scale=a[:, c, bass.ds(pp * G + j // C, 1)]).then_inc(s_dA, 1)
                        if j >= BEHIND or not first:
                            keep_last(ch, pp, j - BEHIND)

                for s, per in ((s_Cs, G), (s_dA, U), (s_hl, U)):
                    act.sem_inc(s, per)
                for ch in range(CHS):
                    act.wait_ge(s_cr, ch + 1)
                    for c in range(C):
                        act.wait_ge(s_xp, ch * C + c + 1)
                        act.copy(xpad[:, c, TAPS - 1:], psum[c][:, :]).then_inc(s_xe, 1)
                    for c in range(C):
                        act.wait_ge(s_cv, ch * C + c + 1)
                        act.activation(xc[:, c, :], conv[:, c % 2, :], ACT.Silu, bias=cb[:, c:c + 1]).then_inc(s_xc, 1)
                    act.wait_ge(s_xd, ch + 1)
                    act.copy(dtl[0:DTR, :], psum[0][2 * S:ROWS, :]).then_inc(s_dl, 1)
                    act.wait_ge(s_dp, ch + 1)
                    act.activation(e[:, :], dt_banks, ACT.Abs).then_inc(s_ab, 1)
                    act.wait_ge(s_ab, ch + 1)
                    act.activation(e[:, :], e[:, :], ACT.Exp, scale=-1.0).then_inc(s_e, 1)
                    act.wait_ge(s_bs, ch * 3 + 3)
                    act.copy(bc3[2 * S:4 * S, :], mid[:, :]).then_inc(s_md, 1)
                    act.wait_ge(s_u, ch + 1)
                    act.activation(delta[:, :], u[:, :], ACT.Ln).then_inc(s_ln, 1)
                    for c in range(C):
                        act.wait_ge(s_zp, ch * C + c + 1)
                        act.activation(sz[:, c, :], bankZ[c][:, :], ACT.Silu).then_inc(s_ze, 1)
                    act.wait_ge(s_dx, ch + 1)
                    if ch == 0:
                        act.wait_ge(s_in, 1)
                    decays(ch, 0, True)
                    with act.Fori(1, STEPS) as pp:
                        decays(ch, pp, False)
                    for i in range(U - BEHIND, U):
                        keep_last(ch, STEPS - 1, i)

            @block.vector
            def _(dve):
                dve.memset(dtl[:, :], 1.0).then_inc(s_z, 1)
                dve.memset(xpad[:, :, 0:TAPS - 1], 0.0).then_inc(s_cr, 1)
                norm.dve(dve)
                dve.wait_ge(s_w, NW * 16)
                for c in range(C):
                    dve.tensor_scalar(skipd[:, c, :], consts["ident"][:, :], skip[:, c:c + 1], None, ALU.mult).then_inc(s_z, 1)
                dve.wait_ge(s_a, 1)
                dve.tensor_scalar(a[:, :, :], a[:, :, :], -1.0, None, ALU.mult).then_inc(s_z, 1)
                dve.wait_ge(s_z, C + 2)
                norm.wait(dve)
                dve.sem_inc(s_in, 1)
                for s, per in ((s_db, U), (s_h, U), (s_xa, 2)):
                    dve.sem_inc(s, per)
                def convolve(ch, c):
                    dve.wait_ge(s_xe, ch * C + c + 1)
                    if ch * C + c >= 2:
                        dve.wait_ge(s_xc, ch * C + c - 1)
                    for k in range(TAPS):
                        src = xpad[:, c, k:k + BLK]
                        acc = conv[:, c % 2, :]
                        if k == 0:
                            ins = dve.tensor_scalar(acc, src, cw[:, c, 0:1], None, ALU.mult)
                        else:
                            dve.wait_ge(s_cs, (ch * C + c) * (TAPS - 1) + k)
                            ins = dve.scalar_tensor_tensor(out=acc, in0=src, scalar=cw[:, c, k:k + 1], in1=acc,
                                                           op0=ALU.mult, op1=ALU.add)
                        ins.then_inc(s_cs if k < TAPS - 1 else s_cv, 1)

                for c in range(C):
                    convolve(0, c)
                for ch in range(CHS):
                    if ch % NCH == 0:
                        dve.wait_ge(s_hl, ch * STEPS * U + U)
                        dve.memset(last[:, :, :], 0.0).then_inc(s_z, 1)
                        dve.wait_ge(s_z, C + 3 + ch // NCH)
                    dve.wait_ge(s_cv, ch * C + C)
                    if ch % NCH < NCH - 1:
                        dve.tensor_copy(xpad[:, :, 0:TAPS - 1], xpad[:, :, BLK:]).then_inc(s_cr, 1)
                    else:
                        dve.memset(xpad[:, :, 0:TAPS - 1], 0.0).then_inc(s_cr, 1)
                    dve.wait_ge(s_xd, ch + 1)
                    bc = psum[0][0:2 * S, :]
                    dve.tensor_copy(bc3[0:2 * S, :], bc).then_inc(s_bs, 1)
                    dve.wait_ge(s_bs, ch * 3 + 1)
                    dve.tensor_tensor(left[:, :], bc, bc3[0:2 * S, :], ALU.subtract).then_inc(s_bs, 1)
                    dve.wait_ge(s_bs, ch * 3 + 2)
                    dve.tensor_copy(mid[:, :], left[:, :]).then_inc(s_bs, 1)
                    dve.wait_ge(s_bs, ch * 3 + 3)
                    dve.tensor_tensor(bc3[4 * S:6 * S, :], left[:, :], mid[:, :], ALU.subtract).then_inc(s_b3, 1)
                    dve.wait_ge(s_dp, ch + 1)
                    dve.wait_ge(s_ab, ch + 1)
                    dve.tensor_scalar(pos[:, :], dt_banks, 0.0, None, ALU.max).then_inc(s_ps, 1)
                    dve.wait_ge(s_e, ch + 1)
                    dve.tensor_scalar(u[:, :], e[:, :], 1.0, None, ALU.add).then_inc(s_u, 1)
                    dve.wait_ge(s_u, ch + 1)
                    dve.scalar_tensor_tensor(out=e[:, :], in0=u[:, :], scalar=1.0, in1=e[:, :], op0=ALU.subtract,
                                             op1=ALU.subtract).then_inc(s_de, 1)
                    dve.wait_ge(s_de, ch * 3 + 1)
                    dve.wait_ge(s_ps, ch + 1)
                    dve.tensor_tensor(pos[:, :], pos[:, :], e[:, :], ALU.subtract).then_inc(s_de, 1)
                    dve.wait_ge(s_de, ch * 3 + 2)
                    dve.wait_ge(s_ln, ch + 1)
                    dve.tensor_tensor(delta[:, :], delta[:, :], pos[:, :], ALU.add).then_inc(s_de, 1)
                    dve.wait_ge(s_de, ch * 3 + 3)
                    dve.tensor_tensor(dx[:, :], delta[:, :], xc[:, :, :].rearrange("p c t -> p (c t)"),
                                      ALU.mult).then_inc(s_dx, 1)
                    dve.wait_ge(s_dx, ch + 1)
                    alone(dve, mark)
                    with dve.Fori(0, STEPS) as pp:
                        q = ch * STEPS + pp + 1

                        def state_input(j):
                            if j % C == 0:
                                dve.wait_ge(s_B, q * G + j // C + 1)
                            dve.wait_ge(s_h, q * U + j - 3)
                            dve.tensor_tensor(inp[:, j % 4, :], dx[:, j % C * BLK:(j % C + 1) * BLK],
                                              bankB[:, :], ALU.mult).then_inc(s_db, 1)

                        state_input(0)
                        for j in range(U):
                            if j + 1 < U:
                                state_input(j + 1)
                            dve.wait_ge(s_dA, q * U + j + 1)
                            dve.wait_ge(s_db, q * U + j + 1)
                            dve.wait_ge(s_hc, q * U + j - 3)
                            dve.wait_ge(s_hl, q * U + j - 3)
                            dve.tensor_tensor_scan(h[:, j % 4, :], bankA[j % 2][:, :], inp[:, j % 4, :],
                                                   last[:, j % C, bass.ds(pp * G + j // C, 1)], ALU.mult,
                                                   ALU.add).then_inc(s_h, 1)
                    for c in range(C):
                        dve.wait_ge(s_y, (ch + 1) * STEPS * U + U - C + c + 1)
                        dve.tensor_tensor(ys[:, c, :], bankY[c][:, :], sz[:, c, :], ALU.mult).then_inc(s_ys, 1)
                    if ch + 1 < CHS:
                        for c in range(C):
                            convolve(ch + 1, c)
                    for t in range(TB // 2):
                        dve.wait_ge(s_op, ch * 2 + t + 1)
                        xt = x[:, ch * TB + 2 * t:ch * TB + 2 * t + 2, :]
                        dve.tensor_tensor(xt, xt, bankO[t][:, :].rearrange("p (t d) -> p t d", t=2), ALU.add).then_inc(s_xa, 1)


def constants(nc, pool, x, x_dram, w):
    c = {
        "ident": pool.sb("ident", [P, P]),
        "ident_bf": pool.sb("ident_bf", [P, P], BF16),
        "row_index": pool.sb("row_index", [P, 1]),
        "eps": pool.sb("eps", [P, 1]),
    }
    s_x = pool.sem("x_loaded")
    s_c = pool.sem("cleared")
    s_k = pool.sem("constants_built")
    with nc.Block() as block:
        @block.sync
        def _(sp):
            sp.dma_start(x[:, :, :], x_dram.rearrange("(t p) d -> p t d", p=P)).then_inc(s_x, 16)
            sp.wait_ge(s_x, 16)

        @block.gpsimd
        def _(pl):
            pl.memset(c["ident"][:, :], 0.0).then_inc(s_c, 1)
            pl.memset(c["ident_bf"][:, :], 0.0).then_inc(s_c, 1)
            pl.wait_ge(s_c, 2)
            for name in ("ident", "ident_bf"):
                pl.affine_select(out=c[name][:, :], in_=c[name][:, :], pattern=[[-1, P]], compare_op=ALU.not_equal,
                                 fill=1.0, base=0, channel_multiplier=1).then_inc(s_k, 1)
            pl.iota(c["row_index"][:, :], pattern=[[0, 1]], base=0, channel_multiplier=1,
                    allow_small_or_imprecise_dtypes=True).then_inc(s_k, 1)
            pl.memset(c["eps"][:, :], EPS).then_inc(s_k, 1)
            pl.wait_ge(s_k, 4)
    return c


def program(nc, a, out):
    with ExitStack() as ctx:
        pool = Pools(nc, ctx, "all")
        x = pool.sb("x", [P, NT, D])
        psum = Banks(ctx.enter_context(nc.psum_tensor("banks", [P, 8, BLK], F32)))
        consts = constants(nc, pool, x, a["x"], a)
        w0 = {k[3:]: v for k, v in a.items() if k.startswith("f0_")}
        w1 = {k[3:]: v for k, v in a.items() if k.startswith("f1_")}
        wa = {k[3:]: v for k, v in a.items() if k.startswith("at_")}
        wm = {k[3:]: v for k, v in a.items() if k.startswith("mb_")}
        for s, stage in enumerate(STAGES or ("F0", "A", "F0", "F1", "M", "F1")):
            if stage == "F0":
                grouped_ffn(nc, f"gffn{s}", x, psum, consts, w0)
            elif stage == "A":
                attention(nc, f"attn{s}", x, psum, consts, wa)
            elif stage == "M":
                mamba(nc, f"mamba{s}", x, psum, consts, wm)
            elif stage == "F1":
                routed_ffn(nc, f"rffn{s}", x, psum, consts, w1)
        s_out = pool.sem("x_stored")
        with nc.Block() as block:
            @block.sync
            def _(sp):
                sp.dma_start(out.rearrange("(t p) d -> p t d", p=P), x[:, :, :]).then_inc(s_out, 16)
                sp.wait_ge(s_out, 16)


def kernel(**inputs):
    import concourse.bacc as _bacc
    from concourse.bass_utils import run_bass_kernel_spmd as _run

    i = {k: np.asarray(v) for k, v in inputs.items()}
    arrays = {
        "x": i["L0_attn_hidden_states"].reshape(N, D),
        "f0_gate_w": i["L0_ffn_gate_w"].T,
        "f0_mask_up_w": i["L0_ffn_mask_up_w"].transpose(1, 0, 2).reshape(D, -1),
        "f0_gate_proj_w": i["L0_ffn_gate_proj_w"].reshape(-1, D).T,
        "f0_up_proj_w": i["L0_ffn_up_proj_w"].reshape(-1, D).T,
        "f0_down_proj_w": i["L0_ffn_down_proj_w"].transpose(0, 2, 1).reshape(-1, D),
        "f0_inv_map": np.tile(i["L0_ffn_inv_map"].reshape(1, -1), (64, 1)),
    }
    rows = np.arange(NT * 7)
    same = (rows[:, None] % 7 == rows[None, :] % 7)
    arrays.update({
        "f1_gate_w": i["L1_ffn_gate_w"],
        "f1_expert_bias": np.tile(i["L1_ffn_expert_bias"].reshape(1, -1), (P, 1)),
        "f1_w1": np.concatenate([i["L1_ffn_shared_w1"], i["L1_ffn_routed_w1"]]).reshape(-1, D),
        "f1_w2": np.concatenate([i["L1_ffn_shared_w2"], i["L1_ffn_routed_w2"]]).reshape(-1, D),
        "f1_same_expert": same.astype(np.float32),
        "f1_earlier_tile": (same & (rows[:, None] < rows[None, :])).astype(np.float32),
    })
    inv = (1.0 / np.float32(10000.0) ** (np.arange(0, 128, 2, dtype=np.float32) / np.float32(128))).astype(np.float32)
    angle = np.outer(inv, np.arange(L, dtype=np.float32)).astype(np.float32)
    arrays.update({
        "at_gate_w": np.concatenate([i["L0_attn_Wgslc"], i["L0_attn_Wgswa"]]).T,
        "at_wq": i["L0_attn_Wq"].T, "at_wk": i["L0_attn_Wk"].T, "at_wv": i["L0_attn_Wv"].T, "at_wo": i["L0_attn_Wo"].T,
        "at_cos": np.concatenate([np.cos(angle)] * 2).astype(np.float32),
        "at_sin": np.concatenate([np.sin(angle), -np.sin(angle)]).astype(np.float32),
    })
    per_channel = lambda v: v.reshape(4, P).T
    xproj = i["L1_attn_x_proj_w"]
    arrays.update({
        "mb_in_proj_w": i["L1_attn_in_proj_w"].T,
        "mb_x_proj_w": np.concatenate([xproj[16:], xproj[:16]]).T,
        "mb_dt_proj_w": np.concatenate([i["L1_attn_dt_proj_w"].T, i["L1_attn_dt_proj_b"].reshape(1, -1)]),
        "mb_out_proj_w": i["L1_attn_out_proj_w"].T,
        "mb_conv_w": i["L1_attn_conv_w"], "mb_conv_b": per_channel(i["L1_attn_conv_b"]),
        "mb_D": per_channel(i["L1_attn_D"]), "mb_A_log": i["L1_attn_A_log"],
    })
    arrays = {k: np.ascontiguousarray(v) for k, v in arrays.items()}
    nc = _bacc.Bacc("TRN2", target_bir_lowering=False, num_devices=1)
    aps = {k: nc.dram_tensor(f"in_{k}", v.shape, mybir.dt.from_np(v.dtype), kind="ExternalInput").ap()
           for k, v in arrays.items()}
    out = nc.dram_tensor("out_x", (N, D), F32, kind="ExternalOutput").ap()
    program(nc, aps, out)
    r = _run(nc, [{f"in_{k}": v for k, v in arrays.items()}], core_ids=[0])
    return r.results[0]["out_x"].reshape(NB, L, D)
```
